# Optimizing a Trainium2 kernel written in Bass

```python
import numpy as np
import jax
import jax.numpy as jnp

def _softmax(x, axis=-1):
    return jax.nn.softmax(x, axis=axis)

def _gelu(x):
    return jax.nn.gelu(x, approximate=True)

def _silu(x):
    return jax.nn.silu(x)

def _sigmoid(x):
    return jax.nn.sigmoid(x)

def _layernorm(x, axis=-1, eps=1e-05):
    m = jnp.mean(x, axis=axis, keepdims=True)
    v = jnp.var(x, axis=axis, keepdims=True)
    return (x - m) / jnp.sqrt(v + eps)

def _scatter_add(tgt, idx, src, axis=0):
    return tgt.at[idx].add(src)

def _segment_sum(src, seg, n):
    return jax.ops.segment_sum(src, seg, n)
kernel_name = 'mk_adaln_ffn_d2_seqx_r4_490808'

def setup_inputs(seed: int=0):
    np.random.seed(seed)
    _w = jnp.asarray

    def _rec_inputs():
        import jax
        import jax.numpy as jnp
        _rk = jax.random.key(seed)
        x = -0.000125 + 0.9999 * jax.random.normal(jax.random.fold_in(_rk, 1), (64, 64, 1024), jnp.float32)
        _lenS = 64 - jax.random.randint(jax.random.fold_in(_rk, 7), (64,), 0, max(1, 64 // 4) + 1, jnp.int32)
        _lenS2 = 64 - jax.random.randint(jax.random.fold_in(_rk, 8), (64,), 0, max(1, 64 // 4) + 1, jnp.int32)
        cond_128 = 0.0061147 + 1.02565 * jax.random.normal(jax.random.fold_in(_rk, 11), (64, 128), jnp.float32)
        fside_S_0 = -0.022604 + 0.987366 * jax.random.normal(jax.random.fold_in(_rk, 12), (64,), jnp.float32)
        return (x, cond_128, fside_S_0)
    x, cond_128, fside_S_0 = _rec_inputs()

    def _L0_cond_setup():
        import jax, jax.numpy as jnp
        import numpy as np
        K = 8
        T = 1.0
        D_EMBD = 128
        IN_C = 64
        OUT_C = 64
        BS = 32
        H = 1024
        HID = 128
        key = jax.random.key(seed)
        ks = jax.random.split(key, 10)
        s = lambda fan_in: 1.0 / np.sqrt(fan_in)
        return {'x': jax.random.normal(ks[0], (BS, IN_C, H), dtype=jnp.float32), 'embedding': jax.random.normal(ks[1], (BS, D_EMBD), dtype=jnp.float32), 'W0': jax.random.normal(ks[2], (D_EMBD, HID), dtype=jnp.float32) * s(D_EMBD), 'b0': jnp.zeros((HID,), dtype=jnp.float32), 'W1': jax.random.normal(ks[3], (HID, HID), dtype=jnp.float32) * s(HID), 'b1': jnp.zeros((HID,), dtype=jnp.float32), 'W2': jax.random.normal(ks[4], (HID, K), dtype=jnp.float32) * s(HID), 'b2': jnp.zeros((K,), dtype=jnp.float32), 'weight': jax.random.normal(ks[5], (K, OUT_C, IN_C, 1), dtype=jnp.float32) * s(IN_C), 'bias_k': jax.random.normal(ks[6], (K, OUT_C), dtype=jnp.float32) * 0.1}
    _L0_cond_all = _L0_cond_setup()
    _L0_cond_in = {k: v for k, v in _L0_cond_all.items() if k in ('W0', 'b0', 'W1', 'b1', 'W2', 'b2', 'weight', 'bias_k')}
    del _L0_cond_all

    def _L0_ffn_setup():
        import jax, jax.numpy as jnp
        import numpy as np
        FP8_MAX = 448.0

        def quantize_tensorwise(x):
            amax = jnp.max(jnp.abs(x))
            inv_scale = jnp.maximum(amax, jnp.asarray(1e-12, x.dtype)) / FP8_MAX
            q = (x / inv_scale).astype(jnp.float8_e4m3fn)
            return (q, inv_scale)
        key = jax.random.key(seed)
        k1, k2, k3 = jax.random.split(key, 3)
        x = jax.random.normal(k1, (4, 256, 1024), dtype=jnp.float32)
        weight = jax.random.normal(k2, (1024, 1024), dtype=jnp.float32) * 0.02
        bias = jax.random.normal(k3, (1024,), dtype=jnp.float32)
        return {'x': x, 'weight': weight, 'bias': bias}
    _L0_ffn_all = _L0_ffn_setup()
    _L0_ffn_in = {k: v for k, v in _L0_ffn_all.items() if k in ('weight', 'bias')}
    del _L0_ffn_all

    def _L1_cond_setup():
        import jax, jax.numpy as jnp
        import numpy as np
        from jax import lax
        N, C_IN, L = (32, 64, 1024)
        C_OUT, K, GROUPS = (64, 9, 4)
        C_DIM, PAD, STRIDE = (128, 4, 1)
        key = jax.random.key(seed)
        k1, k2, k3, k4, k5 = jax.random.split(key, 5)
        x = jax.random.normal(k1, (N, C_IN, L), dtype=jnp.float32)
        c = jax.random.normal(k2, (N, C_DIM), dtype=jnp.float32)
        weight = jax.random.normal(k3, (C_OUT, C_IN // GROUPS, K), dtype=jnp.float32)
        c_weight = jax.random.normal(k4, (C_OUT, C_DIM), dtype=jnp.float32)
        bias = jax.random.normal(k5, (C_OUT,), dtype=jnp.float32)
        return {'x': x, 'c': c, 'weight': weight, 'c_weight': c_weight, 'bias': bias}
    _L1_cond_all = _L1_cond_setup()
    _L1_cond_in = {k: v for k, v in _L1_cond_all.items() if k in ('weight', 'c_weight')}
    del _L1_cond_all

    def _L1_ffn_setup():
        import jax, jax.numpy as jnp
        import numpy as np
        NBITS = 4
        GROUP_SIZE = 128

        def _dequant(W_q, scale, zero):
            N, K = W_q.shape
            G = K // GROUP_SIZE
            Wg = W_q.reshape(N, G, GROUP_SIZE).astype(jnp.float16)
            Wd = (Wg - zero[:, :, None]) * scale[:, :, None]
            return Wd.reshape(N, K)
        key = jax.random.key(seed)
        k1, k2, k3, k4, k5 = jax.random.split(key, 5)
        B, S, K, N = (2, 512, 1024, 1024)
        G = K // GROUP_SIZE
        x = jax.random.normal(k1, (B, S, K), dtype=jnp.float16)
        W_q = jax.random.randint(k2, (N, K), 0, 2 ** NBITS, dtype=jnp.int32)
        scale = (jax.random.uniform(k3, (N, G), dtype=jnp.float32) * 0.01 + 0.001).astype(jnp.float16)
        zero = (jax.random.uniform(k4, (N, G), dtype=jnp.float32) * 2 ** NBITS).astype(jnp.float16)
        bias = jax.random.normal(k5, (N,), dtype=jnp.float16)
        return {'x': x, 'W_q': W_q, 'scale': scale, 'zero': zero, 'bias': bias}
    _L1_ffn_all = _L1_ffn_setup()
    _L1_ffn_in = {k: v for k, v in _L1_ffn_all.items() if k in ('W_q', 'scale', 'zero', 'bias')}
    del _L1_ffn_all
    return {'x': x, 'cond_128': cond_128, 'fside_S_0': fside_S_0, 'L0_cond_W0': _L0_cond_in['W0'], 'L0_cond_b0': _L0_cond_in['b0'], 'L0_cond_W1': _L0_cond_in['W1'], 'L0_cond_b1': _L0_cond_in['b1'], 'L0_cond_W2': _L0_cond_in['W2'], 'L0_cond_b2': _L0_cond_in['b2'], 'L0_cond_weight': _L0_cond_in['weight'], 'L0_cond_bias_k': _L0_cond_in['bias_k'], 'L0_ffn_weight': _L0_ffn_in['weight'], 'L0_ffn_bias': _L0_ffn_in['bias'], 'L1_cond_weight': _L1_cond_in['weight'], 'L1_cond_c_weight': _L1_cond_in['c_weight'], 'L1_ffn_W_q': _L1_ffn_in['W_q'], 'L1_ffn_scale': _L1_ffn_in['scale'], 'L1_ffn_zero': _L1_ffn_in['zero'], 'L1_ffn_bias': _L1_ffn_in['bias']}

def reference(x, cond_128, fside_S_0, L0_cond_W0, L0_cond_b0, L0_cond_W1, L0_cond_b1, L0_cond_W2, L0_cond_b2, L0_cond_weight, L0_cond_bias_k, L0_ffn_weight, L0_ffn_bias, L1_cond_weight, L1_cond_c_weight, L1_ffn_W_q, L1_ffn_scale, L1_ffn_zero, L1_ffn_bias):
    import jax
    import jax.numpy as jnp

    def _L0_cond_ref(x, embedding, W0, b0, W1, b1, W2, b2, weight, bias_k):
        import jax, jax.numpy as jnp
        import numpy as np
        K = 8
        T = 1.0
        D_EMBD = 128
        IN_C = 64
        OUT_C = 64
        BS = 32
        H = 1024
        HID = 128
        h = jax.nn.gelu(embedding @ W0 + b0, approximate=False)
        h = jax.nn.gelu(h @ W1 + b1, approximate=False)
        att = jax.nn.softmax((h @ W2 + b2) / T, axis=-1)
        agg_w = jnp.einsum('bk,koi->boi', att, weight[..., 0])
        agg_b = att @ bias_k
        out = jnp.einsum('boi,bih->boh', agg_w, x) + agg_b[:, :, None]
        return out

    def _L0_ffn_ref(x, weight, bias):
        import jax, jax.numpy as jnp
        import numpy as np
        FP8_MAX = 448.0

        def quantize_tensorwise(x):
            amax = jnp.max(jnp.abs(x))
            inv_scale = jnp.maximum(amax, jnp.asarray(1e-12, x.dtype)) / FP8_MAX
            q = (x / inv_scale).astype(jnp.float8_e4m3fn)
            return (q, inv_scale)
        out_shape = (*x.shape[:-1], weight.shape[0])
        xm = x.reshape(-1, x.shape[-1])
        fp8_x, x_inv_scale = quantize_tensorwise(xm)
        fp8_wt, w_inv_scale = quantize_tensorwise(weight.T)
        acc = jnp.matmul(fp8_x.astype(jnp.float32), fp8_wt.astype(jnp.float32))
        out = acc * (x_inv_scale * w_inv_scale) + bias.astype(jnp.float32)
        return out.reshape(out_shape).astype(x.dtype)

    def _L1_cond_ref(x, c, weight, c_weight, bias):
        import jax, jax.numpy as jnp
        import numpy as np
        from jax import lax
        N, C_IN, L = (32, 64, 1024)
        C_OUT, K, GROUPS = (64, 9, 4)
        C_DIM, PAD, STRIDE = (128, 4, 1)
        out = lax.conv_general_dilated(x, weight, window_strides=(STRIDE,), padding=[(PAD, PAD)], dimension_numbers=('NCH', 'OIH', 'NCH'), feature_group_count=GROUPS)
        ctx = jnp.einsum('nd,od->no', c, c_weight)
        out = out + ctx[:, :, None] + bias[None, :, None]
        return out

    def _L1_ffn_ref(x, W_q, scale, zero, bias):
        import jax, jax.numpy as jnp
        import numpy as np
        NBITS = 4
        GROUP_SIZE = 128

        def _dequant(W_q, scale, zero):
            N, K = W_q.shape
            G = K // GROUP_SIZE
            Wg = W_q.reshape(N, G, GROUP_SIZE).astype(jnp.float16)
            Wd = (Wg - zero[:, :, None]) * scale[:, :, None]
            return Wd.reshape(N, K)
        W = _dequant(W_q, scale, zero)
        out = jnp.einsum('bsk,nk->bsn', x, W)
        return out + bias
    x = x + _L0_ffn_ref(_L0_cond_ref(x, cond_128, L0_cond_W0, L0_cond_b0, L0_cond_W1, L0_cond_b1, L0_cond_W2, L0_cond_b2, L0_cond_weight, L0_cond_bias_k), L0_ffn_weight, L0_ffn_bias)
    x = x + _L1_ffn_ref(_L1_cond_ref(x, cond_128, L1_cond_weight, L1_cond_c_weight, fside_S_0), L1_ffn_W_q, L1_ffn_scale, L1_ffn_zero, L1_ffn_bias)
    return x

_drawn_inputs = setup_inputs


def setup_inputs(seed=0):
    import zlib

    import numpy as np

    out = dict(_drawn_inputs(seed))
    spreads = {'L0_cond_b0': (0.0, 0.8), 'L0_cond_b1': (0.0, 2.0), 'L0_cond_b2': (0.0, 2.0)}
    factors = {'L0_cond_W0': 5.959,
     'L0_cond_W1': 5.412,
     'L0_cond_W2': 5.12,
     'L0_cond_bias_k': 8.0,
     'L1_ffn_bias': 7.382}
    for name, (base, spread) in spreads.items():
        noise = np.random.default_rng([zlib.crc32(name.encode()), seed]).standard_normal(out[name].shape)
        drawn = base * np.exp(spread * noise) if base else spread * noise
        out[name] = jnp.asarray(drawn.astype(out[name].dtype))
    for name, factor in factors.items():
        out[name] = (out[name] * factor).astype(out[name].dtype)
    return out
```

```python
import concourse.bass as bass
from concourse import mybir
from contextlib import ExitStack


def adaln_ffn_kernel(nc, x, cond, fside, cw0, cb0, cw1, cb1, cw2, cb2, cwk, cbk,
                     f0w, f0b, convw, ctxw, f1q, f1s, f1z, f1b, out):
    fp32, bf16, fp16, i32 = mybir.dt.float32, mybir.dt.bfloat16, mybir.dt.float16, mybir.dt.int32
    ALU, ACT, AX = mybir.AluOpType, mybir.ActivationFunctionType, mybir.AxisListType

    B, C, L = x.shape
    P = 128
    T = B * C // P
    NB = P // C
    K = cwk.shape[0]
    D = cond.shape[1]
    CG, TAPS = convw.shape[1], convw.shape[2]
    G = C // CG
    R8 = P // CG
    S = L // R8
    PAD = TAPS // 2
    KT = L // P
    NG = f1s.shape[1]
    H = 512
    BG = NB * G
    SW = S + 2
    FP8_MAX, FP8_STEP = 448.0, 2.0 ** 20
    assert (T, KT, R8, S, BG, D, L) == (32, 8, 8, 128, 8, P, 2 * H)

    x_t = x.rearrange("(t b) c l -> t (b c) l", b=NB)
    out_t = out.rearrange("(t b) c l -> t (b c) l", b=NB)

    ctx = ExitStack()
    with ctx:
        def sb(name, shape, dt):
            return ctx.enter_context(nc.sbuf_tensor(name, shape, dt))

        def sem(name):
            return ctx.enter_context(nc.semaphore(name))

        row_bias_d = nc.dram_tensor("row_bias", (T, P), fp32, kind="Internal").ap()
        row_ctx_d = nc.dram_tensor("row_ctx", (T, P), fp32, kind="Internal").ap()
        split_d = nc.dram_tensor("split_rows", (2, P, R8 * SW * 2), fp16, kind="Internal").ap()

        Y = sb("Y", [P, (T + 2) * L], fp32)
        f0T = sb("f0T", [P, KT, L], bf16)
        f1T = sb("f1T", [P, KT, L], fp16)
        work = sb("work", [P, 7200], fp32)
        bias0 = sb("bias0", [P, L], fp32)
        bias1 = sb("bias1", [P, L], fp16)
        taps16 = sb("taps16", [P, 2, 2, C, R8], fp16)
        rowvec = sb("rowvec", [P, 2, P], fp32)
        ident = sb("ident", [P, P], fp32)
        stat = sb("stat", [P, 48], fp32)

        def slot(n, k=1):
            return Y[:, n * L:(n + k) * L]

        def slot_dyn(t):
            return Y[:, bass.ds(t * L, L)]

        def held(eng, value):
            return value if isinstance(value, int) else eng.snap(value)

        def mixw_dyn(t):
            return work[:, bass.ds(t * P, P)]

        mixw = work[:, 0:T * P].rearrange("p (t m) -> p t m", t=T)
        xring = [slot(0), slot(1), work[:, T * P:T * P + L], work[:, T * P + L:T * P + 2 * L]]
        wk = Y[0:K, 3 * L:7 * L].rearrange("k (o i) -> k o i", i=C)
        tapsf = slot(7).rearrange("p (o w) -> p o w", w=2 * R8)
        wz = slot(8)
        mlp = slot(9)
        w1c = slot(10, 4).bitcast(fp16).rearrange("p (n l) -> p n l", n=KT)
        w0c = slot(14, 4).bitcast(bf16).rearrange("p (r l) -> p r l", r=R8)
        w1i = slot(18, 8).bitcast(i32).rearrange("p (n l) -> p n l", n=KT)
        w0f = slot(26, 8).rearrange("p (r l) -> p r l", r=R8)
        mw0, mw1 = mlp[:, 0:128], mlp[:, 128:256]
        emb, ctw = mlp[0:B, 256:384], mlp[0:C, 384:512]
        embT, ctwT = mlp[:, 512:576], mlp[:, 576:640]
        h0T, h1T = mlp[:, 640:704], mlp[:, 704:768]
        mw2 = mlp[:, 768:776]
        att = mlp[0:B, 776:784]
        attT = mlp[0:K, 784:848]
        mbk = mlp[0:K, 848:912]
        rowb = mlp[0:1, 912:920]
        rowf = mlp[0:1, 920:984]
        mb0, mb1 = mlp[:, 984:985], mlp[:, 985:986]
        ex = mlp[0:B, 986:994]
        mixb = work[0:B, 7000:7064]
        mixc = work[0:B, 7064:7128]
        zs = taps16[:, 0, 0, 0:16, :].rearrange("p a b -> p (a b)")
        zero16, scale16 = zs[:, 0:KT * NG].rearrange("p (n g) -> p n g", g=NG), \
            zs[:, KT * NG:2 * KT * NG].rearrange("p (n g) -> p n g", g=NG)

        qz = work[:, 0:L]
        qT = [work[:, L + n * H:L + (n + 1) * H].bitcast(bf16).rearrange("p (k m) -> p k m", k=KT) for n in range(2)]
        o = 2 * L
        split = work[:, o:o + R8 * SW].bitcast(fp16).rearrange("p (r s e) -> p r s e", r=R8, e=2)
        o += R8 * SW
        convin = work[:, o:o + BG * SW].bitcast(fp16).rearrange("p (g s e) -> p g s e", g=BG, e=2)
        o += BG * SW
        y1 = work[:, o:o + L].rearrange("p (b r m) -> p b r m", b=NB, r=R8)
        o += L
        y1s = [work[:, o + n * L:o + (n + 1) * L].bitcast(fp16).rearrange("p (e k m) -> p e k m", e=2, k=KT)
               for n in range(2)]
        assert o + 2 * L <= 7200

        amax_t = stat[:, 0:T]
        part_max, w_part = stat[:, 32:33], stat[:, 33:34]
        x_max, w_max = stat[:, 34:35], stat[:, 35:36]
        x_inv, w_inv = stat[:, 36:37], stat[:, 37:38]
        x_mul, w_mul = stat[:, 38:39], stat[:, 39:40]
        acc_mul = stat[:, 42:43]
        nmax, rsum, rinv = stat[0:B, 43:44], stat[0:B, 44:45], stat[0:B, 45:46]
        w_all, x_all = stat[0:1, 46:47], stat[0:1, 47:48]

        ones = work[0:1, 6400:6400 + P]
        ident_b = Y[:, 2 * L:2 * L + P // 2].bitcast(bf16)
        ident_h = Y[:, 2 * L + P // 2:2 * L + P].bitcast(fp16)

        ps = [ctx.enter_context(nc.psum_tensor(f"ps{n}", [P, H], fp32)) for n in range(8)]

        ld = {n: sem("ld_" + n) for n in ("mlp", "wk", "f0", "f1", "zs", "taps", "b0", "b1")}
        ld_x = [sem(f"ld_x{n}") for n in range(4)]
        ld_rb = [sem(f"ld_rb{n}") for n in range(2)]
        zeroed = sem("zeroed")
        ident_made = sem("ident_made")
        ident_cast = sem("ident_cast")
        mlp_mm = sem("mlp_mm")
        mlp_ev = sem("mlp_ev")
        mix_mm = sem("mix_mm")
        mix_ev = sem("mix_ev")
        rows_out = sem("rows_out")
        taps_split = sem("taps_split")
        w_red = sem("w_red")
        w_chain = sem("w_chain")
        w_pe = sem("w_pe")
        w_step = sem("w_step")
        w0v = sem("w0v")
        w0q = sem("w0q")
        w1d = sem("w1d")
        wT_mm = sem("wT_mm")
        wT_ev = sem("wT_ev")
        mixed = sem("mixed")
        mixed_ev = sem("mixed_ev")
        mixed_red = sem("mixed_red")
        x_pe = sem("x_pe")
        x_step = sem("x_step")
        ld_x2 = [sem(f"ld_x2_{n}") for n in range(2)]
        ld_ctx = [sem(f"ld_ctx{n}") for n in range(2)]
        pads = sem("pads")
        xb_done = sem("xb_done")
        v_done = sem("v_done")
        q_step = sem("q_step")
        q_done = sem("q_done")
        f0_done = sem("f0_done")
        x1_done = sem("x1_done")
        hi_done = sem("hi_done")
        lo_done = sem("lo_done")
        x1b_done = sem("x1b_done")
        split_out = sem("split_out")
        split_in = sem("split_in")
        conv_done = sem("conv_done")
        y1_done = sem("y1_done")
        yhi_done = sem("yhi_done")
        ylo_done = sem("ylo_done")
        f1_done = sem("f1_done")
        res_done = sem("res_done")
        stored = sem("stored")

        block = ctx.enter_context(nc.Block())

        N_MLP = 11

        @block.sync
        def _(sp):
            col = lambda a: a.rearrange("(p a) -> p a", a=1)
            row = lambda a: a.rearrange("(a n) -> a n", a=1)
            for dst, src in ((emb, cond), (mw0, cw0), (mb0, col(cb0)), (mw1, cw1), (mb1, col(cb1)), (mw2, cw2),
                             (rowb, row(cb2)), (mbk, cbk), (ctw, ctxw), (rowf, row(fside))):
                sp.dma_start(dst, src).then_inc(ld["mlp"], 16)
            sp.dma_start(wk, cwk.rearrange("k o i a -> k o (i a)")).then_inc(ld["wk"], 16)
            sp.dma_start(w0f, f0w.rearrange("(s r) l -> s r l", r=R8)).then_inc(ld["f0"], 16)
            sp.dma_start(zero16, f1z.rearrange("(n p) g -> p n g", p=P)).then_inc(ld["zs"], 16)
            sp.dma_start(scale16, f1s.rearrange("(n p) g -> p n g", p=P)).then_inc(ld["zs"], 16)
            sp.dma_start(w1i, f1q.rearrange("(n p) l -> p n l", p=P)).then_inc(ld["f1"], 16)
            sp.dma_start(bias0[:, :], row(f0b).to_broadcast([P, L])).then_inc(ld["b0"], 16)
            sp.dma_start(bias1[:, :], row(f1b).to_broadcast([P, L])).then_inc(ld["b1"], 16)
            for n in range(4):
                sp.dma_start(xring[n], x_t[n]).then_inc(ld_x[n], 16)
            sp.wait_ge(mlp_ev, N_MLP)
            sp.dma_start(row_bias_d.rearrange("t (b o) -> (t b) o", b=NB), mixb).then_inc(rows_out, 16)
            sp.dma_start(row_ctx_d.rearrange("t (b o) -> (t b) o", b=NB), mixc).then_inc(rows_out, 16)
            sp.wait_ge(rows_out, 32)
            for n in range(2):
                sp.dma_start(rowvec[:, n, :], row_bias_d[n:n + 1, :].to_broadcast([P, P])).then_inc(ld_rb[n], 16)

            def settled():
                sp.wait_ge(rows_out, 32)

            def phase1(t, n, more_x, more_rb):
                if more_rb:
                    settled()
                    sp.wait_ge(mixed_ev, 2 * t + 2)
                    sp.dma_start(rowvec[:, n % 2, :], row_bias_d[bass.ds(t + 2, 1), :].to_broadcast([P, P]))\
                        .then_inc(ld_rb[n % 2], 16)
                if more_x:
                    settled()
                    sp.wait_ge(mixed, 2 * t + 2)
                    sp.dma_start(xring[n], x_t[t + 4]).then_inc(ld_x[n], 16)

            with sp.Fori(0, T - 4 - 3, 4) as i:
                for n in range(4):
                    phase1(i + n, n, True, True)
            for n in range(2):
                phase1(T - 4 + n, n, False, True)

            def load_x(t, n):
                sp.dma_start(slot_dyn(t), x_t[t]).then_inc(ld_x2[n], 16)

            def load_ctx(t, n):
                sp.dma_start(rowvec[:, n, :], row_ctx_d[bass.ds(t, 1), :].to_broadcast([P, P]))\
                    .then_inc(ld_ctx[n], 16)

            def store(t):
                settled()
                sp.wait_ge(res_done, 2 * t + 2)
                sp.dma_start(out_t[t], slot_dyn(t)).then_inc(stored, 16)

            def turn(t, n, conv_read):
                both, back = held(sp, 2 * t + 2), held(sp, 16 * t + 16)
                if conv_read is not None:
                    conv_read = held(sp, conv_read)
                sp.wait_ge(lo_done, both)
                sp.dma_start(split_d[n], split.rearrange("p r s e -> p (r s e)")).then_inc(split_out, 16)
                sp.wait_ge(split_out, back)
                if conv_read is not None:
                    sp.wait_ge(conv_done, conv_read)
                sp.dma_start(convin.rearrange("p g s e -> p g (s e)"),
                             split_d[n].rearrange("(g c) (r f) -> (c r) g f", g=BG, r=R8)).then_inc(split_in, 16)

            sp.wait_ge(mixed, 2 * T)
            load_x(0, 0)
            load_x(1, 1)
            sp.wait_ge(mixed_ev, 2 * T)
            load_ctx(0, 0)
            load_ctx(1, 1)
            for t in range(2):
                sp.wait_ge(q_done, t + 1)
                sp.wait_ge(xb_done, t + 1)
                load_x(t + 2, t)
                turn(t, t, 2 * t if t else None)

            def phase2(t, n, more):
                if more:
                    settled()
                    sp.wait_ge(q_done, t + 1)
                    sp.wait_ge(xb_done, t + 1)
                    load_x(t + 2, n)
                settled()
                sp.wait_ge(y1_done, 2 * t - 2)
                load_ctx(t, n)
                turn(t, n, 2 * t)
                store(t - 2)

            with sp.Fori(2, T - 2 - 1, 2) as i:
                for n in range(2):
                    phase2(i + n, n, True)
            for n in range(2):
                phase2(T - 2 + n, n, False)
            for t in (T - 2, T - 1):
                store(t)
            sp.wait_ge(stored, 16 * T)

        @block.gpsimd
        def _(pool):
            nc.gpsimd.memset(ident[:, :], 0.0).then_inc(zeroed, 1)
            nc.gpsimd.memset(ones, 1.0).then_inc(zeroed, 1)
            pool.wait_ge(zeroed, 2)
            nc.gpsimd.affine_select(out=ident[:, :], in_=ident[:, :], compare_op=ALU.not_equal, fill=1.0, base=0,
                                    pattern=[[-1, P]], channel_multiplier=1).then_inc(ident_made, 1)
            nc.gpsimd.memset(tapsf, 0.0).then_inc(zeroed, 1)
            nc.gpsimd.memset(mixw, 0.0).then_inc(zeroed, 1)
            pool.wait_ge(zeroed, 3)
            for r in range(R8):
                q = (r + PAD) % R8
                pool.dma_start(tapsf[r::R8, :, R8 - 1 - q:R8 - 1 - q + TAPS],
                               convw.rearrange("o c k -> c o k")).then_inc(ld["taps"], 16)
            pool.wait_ge(x_step, 4)
            nc.gpsimd.memset(split, 0.0).then_inc(pads, 1)

            def add_bias0(t, n, ge):
                pool.wait_ge(ld["b0"], 16)
                pool.wait_ge(ld_x2[n], ge)
                nc.gpsimd.tensor_tensor(slot_dyn(t), slot_dyn(t), bias0[:, :], ALU.add).then_inc(xb_done, 1)

            def add_bias1(t):
                parts = held(pool, 2 * t + 2)
                pool.wait_ge(ld["b1"], 16)
                pool.wait_ge(lo_done, parts)
                nc.gpsimd.tensor_tensor(slot_dyn(t), slot_dyn(t), bias1[:, :], ALU.add).then_inc(x1b_done, 1)

            add_bias0(0, 0, 16)
            add_bias0(1, 1, 16)
            with pool.Fori(0, T - 2 - 1, 2) as i:
                add_bias1(i)
                add_bias0(i + 2, 0, 8 * i + 32)
                add_bias1(i + 1)
                add_bias0(i + 3, 1, 8 * i + 32)
            add_bias1(T - 2)
            add_bias1(T - 1)

        @block.scalar
        def _(act):
            act.wait_ge(ident_made, 1)
            nc.scalar.copy(ident_b, ident[:, :]).then_inc(ident_cast, 1)
            nc.scalar.copy(ident_h, ident[:, :]).then_inc(ident_cast, 1)
            act.wait_ge(mlp_mm, 1)
            nc.scalar.copy(embT, ps[0][:, 0:B]).then_inc(mlp_ev, 1)
            act.wait_ge(mlp_mm, 2)
            nc.scalar.copy(ctwT, ps[7][:, 0:C]).then_inc(mlp_ev, 1)
            act.wait_ge(ld["mlp"], 160)
            act.wait_ge(mlp_mm, 3)
            nc.scalar.activation(h0T, ps[1][:, 0:B], ACT.Gelu, bias=mb0).then_inc(mlp_ev, 1)
            act.wait_ge(mlp_mm, 4)
            nc.scalar.activation(h1T, ps[2][:, 0:B], ACT.Gelu, bias=mb1).then_inc(mlp_ev, 1)
            act.wait_ge(mlp_ev, 5)
            nc.scalar.activation(ex, ps[3][0:B, 0:K], ACT.Exp, bias=nmax, accum_out=rsum).then_inc(mlp_ev, 1)
            act.wait_ge(mlp_mm, 6)
            nc.scalar.copy(attT, ps[4][0:K, 0:B]).then_inc(mlp_ev, 1)
            act.wait_ge(mlp_mm, 7)
            nc.scalar.copy(mixb, ps[5][0:B, 0:C]).then_inc(mlp_ev, 1)
            act.wait_ge(mlp_mm, 8)
            nc.scalar.copy(mixc, ps[6][0:B, 0:C]).then_inc(mlp_ev, 1)
            act.wait_ge(zeroed, 4)
            for q in range(4):
                act.wait_ge(mix_mm, q + 1)
                for b in range(NB):
                    pr = slice(b * C, (b + 1) * C)
                    src = ps[q][pr, :].rearrange("p (o t) -> p t o", t=T)
                    ev = nc.scalar.copy(mixw[pr, :, b * C + 16 * q:b * C + 16 * q + 16], src)
                ev.then_inc(mix_ev, 1)
            act.wait_ge(w_step, 3)
            for r in range(R8):
                nc.scalar.activation(w0f[:, r, :], w0f[:, r, :], ACT.Copy, scale=w_mul).then_inc(w0v, 1)
            for m in range(2 * KT):
                act.wait_ge(wT_mm, m + 1)
                pb = ps[4 + m % 4][:, :].bitcast(bf16 if m < KT else fp16).rearrange("p (k q) -> p k q", k=KT)
                dst = f0T if m < KT else f1T
                nc.scalar.copy(dst[:, :, (m % KT) * P:(m % KT + 1) * P], pb).then_inc(wT_ev, 1)

            def scaled(t):
                nc.scalar.activation(slot_dyn(t + 2), slot_dyn(t + 2), ACT.Copy, scale=x_mul).then_inc(v_done, 1)

            def hi(t):
                v = slot_dyn(t).rearrange("p (s r) -> p r s", r=R8)
                act.wait_ge(pads, 1)
                for h in range(2):
                    act.wait_ge(x1_done, 2 * t + h + 1)
                    if h == 0:
                        act.wait_ge(split_out, 16 * t)
                    r = slice(4 * h, 4 * h + 4)
                    s0 = h
                    nc.scalar.copy(split[:, r, s0:s0 + S, 0], v[:, r, :]).then_inc(hi_done, 1)

            def yhi(t, n):
                for b in range(NB):
                    act.wait_ge(y1_done, 2 * t + b + 1)
                    nc.scalar.copy(y1s[n][:, 0, :, b * C:(b + 1) * C], y1[:, b, :, :]).then_inc(yhi_done, 1)

            act.wait_ge(x_step, 4)
            scaled(0)
            scaled(1)
            act.wait_ge(pads, 1)
            v0 = slot(0).rearrange("p (s r) -> p r s", r=R8)
            for h in range(2):
                act.wait_ge(x1_done, h + 1)
                r = slice(4 * h, 4 * h + 4)
                nc.scalar.copy(split[:, r, h:h + S, 0], v0[:, r, :]).then_inc(hi_done, 1)
            scaled(2)
            hi(1)
            yhi(0, 0)
            with act.Fori(2, T - 2 - 1, 2) as i:
                for n in range(2):
                    scaled(i + n + 1)
                    hi(i + n)
                    yhi(i + n - 1, 1 - n)
            scaled(T - 1)
            hi(T - 2)
            yhi(T - 3, 1)
            hi(T - 1)
            yhi(T - 2, 0)
            yhi(T - 1, 1)

        def round_e4m3(dve, src, z, dst, step, n0, done):
            nc.vector.tensor_scalar(z.bitcast(i32), src.bitcast(i32), 0x7F800000, 0x00400000,
                                    ALU.bitwise_and, ALU.bitwise_or).then_inc(step, 1)
            dve.wait_ge(step, n0 + 1)
            nc.vector.tensor_scalar(z, z, 1.5 * 2.0 ** -6, FP8_STEP, ALU.max, ALU.mult).then_inc(step, 1)
            dve.wait_ge(step, n0 + 2)
            nc.vector.tensor_tensor(src, src, z, ALU.add).then_inc(step, 1)
            dve.wait_ge(step, n0 + 3)
            nc.vector.tensor_tensor(dst, src, z, ALU.subtract).then_inc(done, 1)

        @block.vector
        def _(dve):
            dve.wait_ge(mlp_mm, 5)
            nc.vector.tensor_reduce(nmax, ps[3][0:B, 0:K], AX.X, ALU.max, negate=True).then_inc(mlp_ev, 1)
            dve.wait_ge(mlp_ev, 6)
            nc.vector.reciprocal(rinv, rsum).then_inc(mlp_ev, 1)
            dve.wait_ge(mlp_ev, 7)
            nc.vector.tensor_scalar(att, ex, rinv, None, ALU.mult).then_inc(mlp_ev, 1)

            def scales(vmax, inv, mul, src, step, n0):
                nc.vector.tensor_scalar(vmax, src, 1e-12, None, ALU.max).then_inc(step, 1)
                dve.wait_ge(step, n0 + 1)
                nc.vector.tensor_scalar(inv, vmax, 1.0 / FP8_MAX, None, ALU.mult).then_inc(step, 1)
                dve.wait_ge(step, n0 + 2)
                nc.vector.reciprocal(mul, inv).then_inc(step, 1)
                dve.wait_ge(step, n0 + 3)

            dve.wait_ge(ld["f0"], 16)
            nc.vector.tensor_reduce(w_part, w0f.rearrange("p r l -> p (r l)"), AX.X, ALU.max,
                                    apply_absolute_value=True).then_inc(w_red, 1)
            dve.wait_ge(w_pe, 1)
            nc.vector.tensor_reduce(w_all, ps[7][0:1, 0:P], AX.X, ALU.max).then_inc(w_red, 1)
            dve.wait_ge(w_pe, 2)
            scales(w_max, w_inv, w_mul, ps[7][:, 128:129], w_step, 0)
            for r in range(R8):
                if r:
                    dve.wait_ge(w0q, r)
                dve.wait_ge(w0v, r + 1)
                round_e4m3(dve, w0f[:, r, :], wz, w0c[:, r, :], w_chain, 3 * r, w0q)
            dve.wait_ge(ld["zs"], 32)
            dve.wait_ge(ld["f1"], 16)
            grp = lambda a: a.rearrange("p (g k) -> p g k", g=NG)
            for n in range(KT):
                nc.vector.tensor_tensor(grp(w1c[:, n, :]), grp(w1i[:, n, :]),
                                        zero16[:, n, :].unsqueeze(2).to_broadcast([P, NG, L // NG]),
                                        ALU.subtract).then_inc(w_chain, 1)
                dve.wait_ge(w_chain, 3 * R8 + n + 1)
                nc.vector.tensor_tensor(grp(w1c[:, n, :]), grp(w1c[:, n, :]),
                                        scale16[:, n, :].unsqueeze(2).to_broadcast([P, NG, L // NG]),
                                        ALU.mult).then_inc(w1d, 1)
            dve.wait_ge(ld["taps"], 16 * R8)
            dve.wait_ge(w1d, KT)
            tv = tapsf.rearrange("p o (h r) -> p h o r", h=2)
            for h in range(2):
                nc.vector.tensor_copy(taps16[:, 0, h, :, :], tv[:, h]).then_inc(taps_split, 1)
            dve.wait_ge(taps_split, 2)
            for h in range(2):
                nc.vector.tensor_tensor(taps16[:, 1, h, :, :], tv[:, h], taps16[:, 0, h, :, :], ALU.subtract)\
                    .then_inc(taps_split, 1)
            dve.wait_ge(taps_split, 4)

            def mixed_tile(t, n, m, rb):
                dve.wait_ge(ld_rb[m], rb)
                for h in range(2):
                    dve.wait_ge(mixed, 2 * t + h + 1)
                    src = ps[2 * m + h][:, :].rearrange("p (k m) -> p k m", m=P)
                    dst = Y[:, bass.ds((t + 2) * L + h * H, H)].rearrange("p (k m) -> p k m", m=P)
                    nc.vector.tensor_tensor(dst, src, rowvec[:, m, :].unsqueeze(1).to_broadcast([P, H // P, P]),
                                            ALU.add).then_inc(mixed_ev, 1)
                dve.wait_ge(mixed_ev, 2 * t + 2)
                nc.vector.tensor_reduce(stat[:, bass.ds(t, 1)], slot_dyn(t + 2), AX.X, ALU.max,
                                        apply_absolute_value=True).then_inc(mixed_red, 1)

            with dve.Fori(0, T - 1, 2) as i:
                for m in range(2):
                    mixed_tile(i + m, m, m, 8 * i + 16)
            dve.wait_ge(mixed_red, T)
            nc.vector.tensor_reduce(part_max, amax_t, AX.X, ALU.max).then_inc(mixed_red, 1)
            dve.wait_ge(x_pe, 1)
            nc.vector.tensor_reduce(x_all, ps[7][0:1, 0:P], AX.X, ALU.max).then_inc(mixed_red, 1)
            dve.wait_ge(x_pe, 2)
            scales(x_max, x_inv, x_mul, ps[7][:, 128:129], x_step, 0)
            nc.vector.tensor_tensor(acc_mul, x_inv, w_inv, ALU.mult).then_inc(x_step, 1)
            dve.wait_ge(x_step, 4)

            def quantise(t, n):
                if not (isinstance(t, int) and t == 0):
                    dve.wait_ge(q_done, t)
                dve.wait_ge(v_done, t + 1)
                round_e4m3(dve, slot_dyn(t + 2), qz, qT[n].rearrange("p k m -> p (k m)"), q_step, 3 * t, q_done)

            def residual0(t):
                v = slot_dyn(t).rearrange("p (s r) -> p r s", r=R8)
                dve.wait_ge(xb_done, t + 1)
                for h in range(2):
                    dve.wait_ge(f0_done, 2 * t + h + 1)
                    r = slice(4 * h, 4 * h + 4)
                    nc.vector.scalar_tensor_tensor(out=v[:, r, :], in0=ps[h][:, :].rearrange("p (r s) -> p r s", r=4),
                                                   scalar=acc_mul, in1=v[:, r, :], op0=ALU.mult, op1=ALU.add)\
                        .then_inc(x1_done, 1)

            def lo(t):
                v = slot_dyn(t).rearrange("p (s r) -> p r s", r=R8)
                for h in range(2):
                    dve.wait_ge(hi_done, 2 * t + h + 1)
                    r = slice(4 * h, 4 * h + 4)
                    s = slice(h, h + S)
                    nc.vector.tensor_tensor(split[:, r, s, 1], v[:, r, :], split[:, r, s, 0], ALU.subtract)\
                        .then_inc(lo_done, 1)

            def add_ctx(t, n, ge, first=False):
                dve.wait_ge(ld_ctx[n], ge)
                for b in range(NB):
                    dve.wait_ge(conv_done, 2 * t + b + 1)
                    if not first:
                        dve.wait_ge(yhi_done, 2 * t - 1 + b)
                        dve.wait_ge(ylo_done, 2 * t - 1 + b)
                    nc.vector.tensor_tensor(y1[:, b, :, :], ps[4 + b][:, :].rearrange("p (m r) -> p r m", r=R8),
                                            rowvec[:, n, b * C:(b + 1) * C].unsqueeze(1).to_broadcast([P, R8, C]),
                                            ALU.add).then_inc(y1_done, 1)

            def ylo(t, n):
                for b in range(NB):
                    dve.wait_ge(yhi_done, 2 * t + b + 1)
                    nc.vector.tensor_tensor(y1s[n][:, 1, :, b * C:(b + 1) * C], y1[:, b, :, :],
                                            y1s[n][:, 0, :, b * C:(b + 1) * C], ALU.subtract).then_inc(ylo_done, 1)

            def residual1(t, h):
                dve.wait_ge(x1b_done, t + 1)
                dve.wait_ge(f1_done, 2 * t + h + 1)
                v = Y[:, bass.ds(t * L + h * H, H)]
                nc.vector.tensor_tensor(v, ps[2 + h][:, :], v, ALU.add).then_inc(res_done, 1)

            quantise(0, 0)
            residual0(0)
            lo(0)
            quantise(1, 1)
            residual0(1)
            lo(1)
            add_ctx(0, 0, 16, True)
            ylo(0, 0)
            quantise(2, 0)

            def step(t, n, ctx_ge, more=True):
                residual0(t)
                lo(t)
                residual1(t - 2, 0)
                add_ctx(t - 1, 1 - n, ctx_ge)
                ylo(t - 1, 1 - n)
                if more:
                    quantise(t + 1, 1 - n)
                residual1(t - 2, 1)

            with dve.Fori(2, T - 2 - 1, 2) as i:
                step(i, 0, 8 * i)
                step(i + 1, 1, 8 * i + 16)
            step(T - 2, 0, 8 * (T - 2))
            step(T - 1, 1, 8 * (T - 2) + 16, False)
            residual1(T - 2, 0)
            add_ctx(T - 1, 1, 8 * T)
            ylo(T - 1, 1)
            residual1(T - 2, 1)
            residual1(T - 1, 0)
            residual1(T - 1, 1)

        @block.tensor
        def _(pe):
            mm = nc.tensor.matmul
            pe.wait_ge(ident_made, 1)
            pe.wait_ge(ld["mlp"], 160)
            nc.tensor.transpose(ps[0][:, 0:B], emb, ident[0:B, 0:B]).then_inc(mlp_mm, 1)
            nc.tensor.transpose(ps[7][:, 0:C], ctw, ident[0:C, 0:C]).then_inc(mlp_mm, 1)
            pe.wait_ge(mlp_ev, 1)
            mm(ps[1][:, 0:B], mw0, embT, start=True, stop=True).then_inc(mlp_mm, 1)
            pe.wait_ge(mlp_ev, 3)
            mm(ps[2][:, 0:B], mw1, h0T, start=True, stop=True).then_inc(mlp_mm, 1)
            pe.wait_ge(mlp_ev, 4)
            mm(ps[3][0:B, 0:K], h1T, mw2, start=True, stop=False)
            mm(ps[3][0:B, 0:K], ones[0:1, 0:B], rowb, start=False, stop=True).then_inc(mlp_mm, 1)
            pe.wait_ge(mlp_ev, 8)
            nc.tensor.transpose(ps[4][0:K, 0:B], att, ident[0:B, 0:B]).then_inc(mlp_mm, 1)
            pe.wait_ge(mlp_ev, 9)
            mm(ps[5][0:B, 0:C], attT, mbk, start=True, stop=True).then_inc(mlp_mm, 1)
            mm(ps[6][0:B, 0:C], embT, ctwT, start=True, stop=False)
            mm(ps[6][0:B, 0:C], ones[0:1, 0:B], rowf, start=False, stop=True).then_inc(mlp_mm, 1)
            pe.wait_ge(ld["wk"], 16)
            for q in range(4):
                for o16 in range(16):
                    for b in range(NB):
                        last = mm(ps[q][b * C:(b + 1) * C, o16 * T:(o16 + 1) * T], wk[:, 16 * q + o16, :],
                                  attT[:, b::NB], start=True, stop=True)
                last.then_inc(mix_mm, 1)
            pe.wait_ge(w_red, 1)
            nc.tensor.transpose(ps[7][0:1, 0:P], w_part, ident[:, :]).then_inc(w_pe, 1)
            pe.wait_ge(w_red, 2)
            mm(ps[7][:, 128:129], ones, w_all, start=True, stop=True).then_inc(w_pe, 1)
            pe.wait_ge(ident_cast, 2)
            pe.wait_ge(w_step, 3)
            pe.wait_ge(mlp_ev, N_MLP)
            for m in range(2 * KT):
                if m >= 4:
                    pe.wait_ge(wT_ev, m - 3)
                r = m % KT
                if m < KT:
                    pe.wait_ge(w0q, r + 1)
                    for k in range(KT):
                        last = nc.tensor.transpose(ps[4 + m % 4][:, :].bitcast(bf16)[:, k * P:(k + 1) * P],
                                                   w0c[:, r, k * P:(k + 1) * P], ident_b)
                else:
                    pe.wait_ge(w1d, r + 1)
                    wv = w1c[:, r, :].rearrange("p (s r) -> p r s", r=R8)
                    for k in range(KT):
                        last = nc.tensor.transpose(ps[4 + m % 4][:, :].bitcast(fp16)[:, k * P:(k + 1) * P],
                                                   wv[:, R8 - 1 - k, :], ident_h)
                last.then_inc(wT_mm, 1)
            pe.wait_ge(mix_ev, 4)

            def mixed_tile(t, n, m, xl, first):
                pe.wait_ge(ld_x[n], xl)
                for h in range(2):
                    if not first:
                        pe.wait_ge(mixed_ev, 2 * t + h - 3)
                    for k in range(4):
                        j = 4 * h + k
                        last = mm(ps[2 * m + h][:, k * P:(k + 1) * P], xring[n][:, j * P:(j + 1) * P],
                                  mixw_dyn(t), start=True, stop=True)
                    last.then_inc(mixed, 1)

            for n in range(4):
                mixed_tile(n, n, n % 2, 16, n < 2)
            with pe.Fori(4, T - 3, 4) as i:
                for n in range(4):
                    mixed_tile(i + n, n, n % 2, 4 * i + 16, False)
            pe.wait_ge(mixed_red, T + 1)
            pe.wait_ge(wT_ev, 2 * KT)
            nc.tensor.transpose(ps[7][0:1, 0:P], part_max, ident[:, :]).then_inc(x_pe, 1)
            pe.wait_ge(mixed_red, T + 2)
            mm(ps[7][:, 128:129], ones, x_all, start=True, stop=True).then_inc(x_pe, 1)
            pe.wait_ge(taps_split, 4)

            def ffn0(t, n, first=False):
                pe.wait_ge(q_done, t + 1)
                for h in range(2):
                    if not first:
                        pe.wait_ge(x1_done, 2 * t - 1 + h)
                    for k in range(KT):
                        last = mm(ps[h][:, :], qT[n][:, k, :], f0T[:, k, h * H:(h + 1) * H],
                                  start=(k == 0), stop=(k == KT - 1))
                    last.then_inc(f0_done, 1)

            def conv(t, first=False):
                pe.wait_ge(split_in, 16 * t + 16)
                for b in range(NB):
                    if not first:
                        pe.wait_ge(y1_done, 2 * t - 1 + b)
                    for g in range(G):
                        parts = [(xp, wp, h) for xp, wp in ((0, 0), (0, 1), (1, 0)) for h in range(2)]
                        for j, (xp, wp, h) in enumerate(parts):
                            last = mm(ps[4 + b][:, g * P:(g + 1) * P], convin[:, b * G + g, h:h + S, xp],
                                      taps16[:, wp, h, g * CG:(g + 1) * CG, :].rearrange("p a b -> p (a b)"),
                                      start=(j == 0), stop=(j == len(parts) - 1))
                    last.then_inc(conv_done, 1)

            def ffn1(t, n, h, first=False):
                pe.wait_ge(ylo_done, 2 * t + 2)
                if not first:
                    pe.wait_ge(res_done, 2 * t - 1 + h)
                for e in range(2):
                    for k in range(KT):
                        last = mm(ps[2 + h][:, :], y1s[n][:, e, k, :], f1T[:, k, h * H:(h + 1) * H],
                                  start=(e == 0 and k == 0), stop=(e == 1 and k == KT - 1))
                last.then_inc(f1_done, 1)

            ffn0(0, 0, True)
            ffn0(1, 1)
            conv(0, True)

            def step(t, n, first=False):
                ffn0(t, n)
                ffn1(t - 2, n, 0, first)
                conv(t - 1)
                ffn1(t - 2, n, 1, first)

            step(2, 0, True)
            step(3, 1)
            with pe.Fori(4, T - 1, 2) as i:
                step(i, 0)
                step(i + 1, 1)
            ffn1(T - 2, 0, 0)
            conv(T - 1)
            ffn1(T - 2, 0, 1)
            ffn1(T - 1, 1, 0)
            ffn1(T - 1, 1, 1)



_INS = ['x', 'cond_128', 'fside_S_0', 'L0_cond_W0', 'L0_cond_b0', 'L0_cond_W1', 'L0_cond_b1', 'L0_cond_W2',
        'L0_cond_b2', 'L0_cond_weight', 'L0_cond_bias_k', 'L0_ffn_weight', 'L0_ffn_bias', 'L1_cond_weight',
        'L1_cond_c_weight', 'L1_ffn_W_q', 'L1_ffn_scale', 'L1_ffn_zero', 'L1_ffn_bias']


def kernel(**inputs):
    import numpy as _np
    import concourse.bacc as _bacc
    from concourse import mybir as _mybir
    from concourse.bass_utils import run_bass_kernel_spmd as _run

    nc = _bacc.Bacc("TRN2", target_bir_lowering=False, num_devices=1)
    arrays, args = {}, []
    for name in _INS:
        a = _np.ascontiguousarray(inputs[name])
        arrays[f"in_{name}_dram"] = a
        args.append(nc.dram_tensor(f"in_{name}_dram", a.shape, _mybir.dt.from_np(a.dtype), kind="ExternalInput").ap())
    out = nc.dram_tensor("out_dram", inputs['x'].shape, _mybir.dt.float32, kind="ExternalOutput").ap()
    adaln_ffn_kernel(nc, *args, out)
    return _run(nc, [arrays], core_ids=[0]).results[0]["out_dram"]
```

```python
import concourse.bass as bass
from concourse import mybir
from contextlib import ExitStack


def adaln_ffn_kernel(nc, x, cond, fside, cw0, cb0, cw1, cb1, cw2, cb2, cwk, cbk,
                     f0w, f0b, convw, ctxw, f1q, f1s, f1z, f1b, out):
    fp32, bf16, fp16, i32 = mybir.dt.float32, mybir.dt.bfloat16, mybir.dt.float16, mybir.dt.int32
    ALU, ACT, AX = mybir.AluOpType, mybir.ActivationFunctionType, mybir.AxisListType

    B, C, L = x.shape
    P = 128
    T = B * C // P
    NB = P // C
    K = cwk.shape[0]
    D = cond.shape[1]
    CG, TAPS = convw.shape[1], convw.shape[2]
    G = C // CG
    R8 = P // CG
    S = L // R8
    PAD = TAPS // 2
    KT = L // P
    NG = f1s.shape[1]
    H = 512
    BG = NB * G
    SW = S + 2
    FP8_MAX, FP8_STEP = 448.0, 2.0 ** 20
    assert (T, KT, R8, S, BG, D, L) == (32, 8, 8, 128, 8, P, 2 * H)

    x_t = x.rearrange("(t b) c l -> t (b c) l", b=NB)
    out_t = out.rearrange("(t b) c l -> t (b c) l", b=NB)

    ctx = ExitStack()
    with ctx:
        def sb(name, shape, dt):
            return ctx.enter_context(nc.sbuf_tensor(name, shape, dt))

        def sem(name):
            return ctx.enter_context(nc.semaphore(name))

        row_bias_d = nc.dram_tensor("row_bias", (3, T, P), bf16, kind="Internal").ap()
        row_ctx_d = nc.dram_tensor("row_ctx", (T, P), fp32, kind="Internal").ap()
        split_d = nc.dram_tensor("split_rows", (2, P, R8 * SW * 2), fp16, kind="Internal").ap()

        Y = sb("Y", [P, (T + 2) * L], fp32)
        f0T = sb("f0T", [P, KT, L], bf16)
        f1T = sb("f1T", [P, KT, L], fp16)
        work = sb("work", [P, 7200], fp32)
        bias0 = sb("bias0", [P, L], fp32)
        bias1 = sb("bias1", [P, L], fp16)
        taps16 = sb("taps16", [P, 2, 2, C, R8], fp16)
        rowvec = sb("rowvec", [P, 2, P], fp32)
        ident = sb("ident", [P, P], fp32)
        stat = sb("stat", [P, 48], fp32)

        def slot(n, k=1):
            return Y[:, n * L:(n + k) * L]

        def slot_dyn(t):
            return Y[:, bass.ds(t * L, L)]

        def mix_src(q, par, b):
            return ps[q][par * C:(par + 1) * C, :].rearrange("p (j t b) -> p b t j", t=T, b=NB)[:, b]

        def mix_dst(q, par, b):
            o = b * C + 16 * q + par
            return mixw[b * C:(b + 1) * C, :, o:o + 15:2]

        def held(eng, value):
            return value if isinstance(value, int) else eng.snap(value)

        def w0c_dyn(r, k):
            return f1T[:, r, k * P:(k + 1) * P].bitcast(bf16)

        def w1c_dyn(n, k):
            base = Y[:, W1C_SLOT * L:(W1C_SLOT + 4) * L].bitcast(fp16)
            return base[:, bass.ds(n * L + R8 - 1 - k, S, R8)]

        def mixw_dyn(t):
            return work[:, bass.ds(t * P, P)]

        mixw = work[:, 0:T * P].rearrange("p (t m) -> p t m", t=T)
        xring = [slot(0), slot(1), work[:, T * P:T * P + L], work[:, T * P + L:T * P + 2 * L]]
        wk = Y[0:K, 3 * L:7 * L].rearrange("k (o i) -> k o i", i=C)
        tapsf = slot(7).rearrange("p (o w) -> p o w", w=2 * R8)
        mlp = slot(9)
        W0_SLOT, W1_SLOT, W1C_SLOT = 14, 22, 30
        w0f = slot(W0_SLOT, 8).rearrange("p (r l) -> p r l", r=R8)
        w1i = slot(W1_SLOT, 8).bitcast(i32).rearrange("p (n l) -> p n l", n=KT)
        w1c = slot(W1C_SLOT, 4).bitcast(fp16).rearrange("p (n l) -> p n l", n=KT)
        w0c = f1T[:, :, :].bitcast(bf16)
        wz = bias0[:, :]
        mw0, mw1 = mlp[:, 0:128], mlp[:, 128:256]
        emb, ctw = mlp[0:B, 256:384], mlp[0:C, 384:512]
        embT, ctwT = mlp[:, 512:576], mlp[:, 576:640]
        h0T, h1T = mlp[:, 640:704], mlp[:, 704:768]
        mw2 = mlp[:, 768:776]
        att = mlp[0:B, 776:784]
        attT = mlp[0:K, 784:848]
        mbk = mlp[0:K, 848:912]
        rowb = mlp[0:1, 912:920]
        rowf = mlp[0:1, 920:984]
        mb0, mb1 = mlp[:, 984:985], mlp[:, 985:986]
        ex = mlp[0:B, 986:994]
        mixb = work[0:B, 7000:7064]
        mixr = work[0:B, 6936:7000]
        mixp = work[0:B, 6600:6696].bitcast(bf16).rearrange("p (e o) -> p e o", e=3)
        mixc = work[0:B, 7064:7128]
        zs = bias1[:, 7 * P:8 * P]
        zero16, scale16 = zs[:, 0:KT * NG].rearrange("p (n g) -> p n g", g=NG), \
            zs[:, KT * NG:2 * KT * NG].rearrange("p (n g) -> p n g", g=NG)

        qz = work[:, 0:L]
        qT = [work[:, L + n * H:L + (n + 1) * H].bitcast(bf16).rearrange("p (k m) -> p k m", k=KT) for n in range(2)]
        o = 2 * L
        split = work[:, o:o + R8 * SW].bitcast(fp16).rearrange("p (r s e) -> p r s e", r=R8, e=2)
        o += R8 * SW
        convin = work[:, o:o + BG * SW].bitcast(fp16).rearrange("p (g s e) -> p g s e", g=BG, e=2)
        o += BG * SW
        y1 = work[:, o:o + L].rearrange("p (b r m) -> p b r m", b=NB, r=R8)
        o += L
        y1s = [work[:, o + n * L:o + (n + 1) * L].bitcast(fp16).rearrange("p (e k m) -> p e k m", e=2, k=KT)
               for n in range(2)]
        assert o + 2 * L <= 7200

        amax_t = stat[:, 0:T]
        part_max, w_part = stat[:, 32:33], stat[:, 33:34]
        w_half = stat[:, 40:42]
        x_max, w_max = stat[:, 34:35], stat[:, 35:36]
        x_inv, w_inv = stat[:, 36:37], stat[:, 37:38]
        x_mul, w_mul = stat[:, 38:39], stat[:, 39:40]
        acc_mul = stat[:, 42:43]
        nmax, rsum, rinv = stat[0:B, 43:44], stat[0:B, 44:45], stat[0:B, 45:46]
        w_all, x_all = stat[0:1, 46:47], stat[0:1, 47:48]

        ones = work[0:1, 6400:6400 + P]
        ident_b = bias1[:, 0:P].bitcast(bf16)
        ident_h = bias1[:, P:2 * P]
        ones_b = bias1[0:3, 2 * P:3 * P].bitcast(bf16)
        rowb3 = bias1[0:3, 3 * P:7 * P].bitcast(bf16).rearrange("p (n m) -> p n m", n=4)

        ps = [ctx.enter_context(nc.psum_tensor(f"ps{n}", [P, H], fp32)) for n in range(8)]

        ld = {n: sem("ld_" + n) for n in ("mlp", "wk", "f0a", "f0b", "zs", "taps", "b0", "b1")}
        ld_f1 = {n: sem(f"ld_f1_{n}") for n in (0, 2, 3, 4, 5, 6, 7)}
        ld_x = [sem(f"ld_x{n}") for n in range(4)]
        ld_rb = [sem(f"ld_rb{n}") for n in range(4)]
        zeroed = sem("zeroed")
        ident_made = sem("ident_made")
        ident_cast = sem("ident_cast")
        mlp_mm = sem("mlp_mm")
        mlp_ev = sem("mlp_ev")
        mix_mm = sem("mix_mm")
        mix_even = sem("mix_even")
        mix_odd = sem("mix_odd")
        bias_parts = sem("bias_parts")
        w1_cast = sem("w1_cast")
        w1_step = sem("w1_step")
        rows_out = sem("rows_out")
        taps_split = sem("taps_split")
        w_red = sem("w_red")
        w_chain = sem("w_chain")
        w_pe = sem("w_pe")
        w_step = sem("w_step")
        w0v = sem("w0v")
        w0q = sem("w0q")
        w1d = sem("w1d")
        wT_mm = sem("wT_mm")
        wT_ev = sem("wT_ev")
        mixed = sem("mixed")
        mixed_ev = sem("mixed_ev")
        mixed_red = sem("mixed_red")
        x_pe = sem("x_pe")
        x_step = sem("x_step")
        ld_x2 = [sem(f"ld_x2_{n}") for n in range(2)]
        ld_ctx = [sem(f"ld_ctx{n}") for n in range(2)]
        pads = sem("pads")
        xb_done = sem("xb_done")
        v_done = sem("v_done")
        q_step = sem("q_step")
        q_done = sem("q_done")
        f0_done = sem("f0_done")
        x1_done = sem("x1_done")
        hi_done = sem("hi_done")
        lo_done = sem("lo_done")
        x1b_done = sem("x1b_done")
        split_out = sem("split_out")
        split_in = sem("split_in")
        conv_done = sem("conv_done")
        y1_done = sem("y1_done")
        yhi_done = sem("yhi_done")
        ylo_done = sem("ylo_done")
        f1_done = sem("f1_done")
        res_done = sem("res_done")
        stored = sem("stored")

        block = ctx.enter_context(nc.Block())

        N_MLP = 11

        @block.sync
        def _(sp):
            col = lambda a: a.rearrange("(p a) -> p a", a=1)
            row = lambda a: a.rearrange("(a n) -> a n", a=1)
            for dst, src in ((emb, cond), (mw0, cw0), (mb0, col(cb0)), (mw1, cw1), (mb1, col(cb1)), (mw2, cw2),
                             (rowb, row(cb2)), (mbk, cbk), (ctw, ctxw), (rowf, row(fside))):
                sp.dma_start(dst, src).then_inc(ld["mlp"], 16)
            sp.dma_start(wk, cwk.rearrange("k o i a -> k o (i a)")).then_inc(ld["wk"], 16)
            f0_rows = f0w.rearrange("(s r) l -> s r l", r=R8)
            sp.dma_start(w0f[:, 0:4, :], f0_rows[:, 0:4, :]).then_inc(ld["f0a"], 16)
            sp.dma_start(w0f[:, 4:8, :], f0_rows[:, 4:8, :]).then_inc(ld["f0b"], 16)
            for n in range(4):
                sp.dma_start(xring[n], x_t[n]).then_inc(ld_x[n], 16)
            sp.dma_start(zero16, f1z.rearrange("(n p) g -> p n g", p=P)).then_inc(ld["zs"], 16)
            sp.dma_start(scale16, f1s.rearrange("(n p) g -> p n g", p=P)).then_inc(ld["zs"], 16)
            sp.wait_ge(mlp_ev, N_MLP)
            sp.wait_ge(bias_parts, 4)
            sp.dma_start(row_bias_d.rearrange("e t (b o) -> (t b) e o", b=NB), mixp).then_inc(rows_out, 16)
            sp.dma_start(row_ctx_d.rearrange("t (b o) -> (t b) o", b=NB), mixc).then_inc(rows_out, 16)
            sp.wait_ge(rows_out, 32)
            for n in range(4):
                sp.dma_start(rowb3[:, n, :], row_bias_d[:, n, :]).then_inc(ld_rb[n], 16)
            f1_rows = f1q.rearrange("(n p) l -> p n l", p=P)

            def load_f1(n, k):
                sp.dma_start(w1i[:, n:n + k, :], f1_rows[:, n:n + k, :]).then_inc(ld_f1[n], 16)

            load_f1(0, 2)

            def settled():
                sp.wait_ge(rows_out, 32)

            def next_tile(t, n):
                settled()
                sp.wait_ge(mixed, 2 * t + 2)
                sp.dma_start(rowb3[:, n, :], row_bias_d[:, bass.ds(t + 4, 1), :]).then_inc(ld_rb[n], 16)
                sp.dma_start(xring[n], x_t[t + 4]).then_inc(ld_x[n], 16)

            for t in range(12):
                next_tile(t, t % 4)
                if t % 2 == 0:
                    load_f1(2 + t // 2, 1)
            with sp.Fori(12, T - 4 - 3, 4) as i:
                for n in range(4):
                    next_tile(i + n, n)

            def load_x(t, n):
                sp.dma_start(slot_dyn(t), x_t[t]).then_inc(ld_x2[n], 16)

            def load_ctx(t, n):
                sp.dma_start(rowvec[:, n, :], row_ctx_d[bass.ds(t, 1), :].to_broadcast([P, P]))\
                    .then_inc(ld_ctx[n], 16)

            def store(t):
                settled()
                sp.wait_ge(res_done, 2 * t + 2)
                sp.dma_start(out_t[t], slot_dyn(t)).then_inc(stored, 16)

            def turn(t, n, conv_read):
                both, back = held(sp, 2 * t + 2), held(sp, 16 * t + 16)
                if conv_read is not None:
                    conv_read = held(sp, conv_read)
                sp.wait_ge(lo_done, both)
                sp.dma_start(split_d[n], split.rearrange("p r s e -> p (r s e)")).then_inc(split_out, 16)
                sp.wait_ge(split_out, back)
                if conv_read is not None:
                    sp.wait_ge(conv_done, conv_read)
                sp.dma_start(convin.rearrange("p g s e -> p g (s e)"),
                             split_d[n].rearrange("(g c) (r f) -> (c r) g f", g=BG, r=R8)).then_inc(split_in, 16)

            load_ctx(0, 0)
            load_ctx(1, 1)
            sp.wait_ge(w0q, R8)
            sp.dma_start(bias0[:, :], row(f0b).to_broadcast([P, L])).then_inc(ld["b0"], 16)
            sp.wait_ge(mixed, 2 * T)
            load_x(0, 0)
            load_x(1, 1)
            sp.wait_ge(w1d, KT)
            sp.dma_start(bias1[:, :], row(f1b).to_broadcast([P, L])).then_inc(ld["b1"], 16)
            for t in range(2):
                sp.wait_ge(q_done, t + 1)
                sp.wait_ge(xb_done, t + 1)
                load_x(t + 2, t)
                turn(t, t, 2 * t if t else None)

            def phase2(t, n, more):
                if more:
                    settled()
                    sp.wait_ge(q_done, t + 1)
                    sp.wait_ge(xb_done, t + 1)
                    load_x(t + 2, n)
                settled()
                sp.wait_ge(y1_done, 2 * t - 2)
                load_ctx(t, n)
                turn(t, n, 2 * t)
                store(t - 2)

            with sp.Fori(2, T - 2 - 1, 2) as i:
                for n in range(2):
                    phase2(i + n, n, True)
            for n in range(2):
                phase2(T - 2 + n, n, False)
            for t in (T - 2, T - 1):
                store(t)
            sp.wait_ge(stored, 16 * T)

        @block.gpsimd
        def _(pool):
            nc.gpsimd.memset(ident[:, :], 0.0).then_inc(zeroed, 1)
            nc.gpsimd.memset(ones, 1.0).then_inc(zeroed, 1)
            pool.wait_ge(zeroed, 2)
            nc.gpsimd.affine_select(out=ident[:, :], in_=ident[:, :], compare_op=ALU.not_equal, fill=1.0, base=0,
                                    pattern=[[-1, P]], channel_multiplier=1).then_inc(ident_made, 1)
            nc.gpsimd.memset(tapsf, 0.0).then_inc(zeroed, 1)
            nc.gpsimd.memset(ones_b, 1.0).then_inc(zeroed, 1)
            pool.wait_ge(zeroed, 3)
            for r in range(R8):
                q = (r + PAD) % R8
                pool.dma_start(tapsf[r::R8, :, R8 - 1 - q:R8 - 1 - q + TAPS],
                               convw.rearrange("o c k -> c o k")).then_inc(ld["taps"], 16)
            nc.gpsimd.memset(mixw, 0.0).then_inc(zeroed, 1)
            grp = lambda a: a.rearrange("p (g k) -> p g k", g=NG)
            wide = lambda a: a.unsqueeze(2).to_broadcast([P, NG, L // NG])
            pool.wait_ge(ld["zs"], 32)
            for n in range(KT):
                pool.wait_ge(w1_cast, n + 1)
                nc.gpsimd.tensor_tensor(grp(w1c[:, n, :]), grp(w1c[:, n, :]), wide(zero16[:, n, :]),
                                        ALU.subtract).then_inc(w1_step, 1)
                pool.wait_ge(w1_step, n + 1)
                nc.gpsimd.tensor_tensor(grp(w1c[:, n, :]), grp(w1c[:, n, :]), wide(scale16[:, n, :]),
                                        ALU.mult).then_inc(w1d, 1)
            pool.wait_ge(x_step, 4)
            nc.gpsimd.memset(split, 0.0).then_inc(pads, 1)

            def add_bias0(t, n, ge):
                pool.wait_ge(ld["b0"], 16)
                pool.wait_ge(ld_x2[n], ge)
                nc.gpsimd.tensor_tensor(slot_dyn(t), slot_dyn(t), bias0[:, :], ALU.add).then_inc(xb_done, 1)

            def add_bias1(t):
                parts = held(pool, 2 * t + 2)
                pool.wait_ge(ld["b1"], 16)
                pool.wait_ge(lo_done, parts)
                nc.gpsimd.tensor_tensor(slot_dyn(t), slot_dyn(t), bias1[:, :], ALU.add).then_inc(x1b_done, 1)

            add_bias0(0, 0, 16)
            add_bias0(1, 1, 16)
            with pool.Fori(0, T - 2 - 1, 2) as i:
                add_bias1(i)
                add_bias0(i + 2, 0, 8 * i + 32)
                add_bias1(i + 1)
                add_bias0(i + 3, 1, 8 * i + 32)
            add_bias1(T - 2)
            add_bias1(T - 1)

        @block.scalar
        def _(act):
            act.wait_ge(ident_made, 1)
            nc.scalar.copy(ident_b, ident[:, :]).then_inc(ident_cast, 1)
            nc.scalar.copy(ident_h, ident[:, :]).then_inc(ident_cast, 1)
            act.wait_ge(mlp_mm, 1)
            nc.scalar.copy(embT, ps[0][:, 0:B]).then_inc(mlp_ev, 1)
            act.wait_ge(mlp_mm, 2)
            nc.scalar.copy(ctwT, ps[7][:, 0:C]).then_inc(mlp_ev, 1)
            act.wait_ge(ld["mlp"], 160)
            act.wait_ge(mlp_mm, 3)
            nc.scalar.activation(h0T, ps[1][:, 0:B], ACT.Gelu, bias=mb0).then_inc(mlp_ev, 1)
            act.wait_ge(mlp_mm, 4)
            nc.scalar.activation(h1T, ps[2][:, 0:B], ACT.Gelu, bias=mb1).then_inc(mlp_ev, 1)
            act.wait_ge(mlp_ev, 5)
            nc.scalar.activation(ex, ps[3][0:B, 0:K], ACT.Exp, bias=nmax, accum_out=rsum).then_inc(mlp_ev, 1)
            act.wait_ge(mlp_mm, 6)
            nc.scalar.copy(attT, ps[4][0:K, 0:B]).then_inc(mlp_ev, 1)
            act.wait_ge(mlp_mm, 7)
            nc.scalar.copy(mixb, ps[5][0:B, 0:C]).then_inc(mlp_ev, 1)
            act.wait_ge(mlp_mm, 8)
            nc.scalar.copy(mixc, ps[6][0:B, 0:C]).then_inc(mlp_ev, 1)
            act.wait_ge(zeroed, 5)
            for q in range(4):
                act.wait_ge(mix_mm, q + 1)
                for b in range(NB):
                    ev = nc.scalar.copy(mix_dst(q, 0, b), mix_src(q, 0, b))
                ev.then_inc(mix_even, 1)

            def keep_mixed(t, m):
                for h in range(2):
                    act.wait_ge(mixed, 2 * t + h + 1)
                    nc.scalar.copy(Y[:, bass.ds((t + 2) * L + h * H, H)], ps[2 * m + h][:, :]).then_inc(mixed_ev, 1)

            def keep_turned(m, dst, dt, at):
                act.wait_ge(wT_mm, at + 1)
                pb = ps[4 + m][:, :].bitcast(dt).rearrange("p (k q) -> p k q", k=KT)
                nc.scalar.copy(dst, pb).then_inc(wT_ev, 1)

            def scale_w0(r):
                wr = Y[:, bass.ds((r + W0_SLOT) * L, L)]
                nc.scalar.activation(wr, wr, ACT.Copy, scale=w_mul).then_inc(w0v, 1)

            def cast_w1(n):
                nc.scalar.copy(w1c[:, n, :], w1i[:, n, :]).then_inc(w1_cast, 1)

            act.wait_ge(w_step, 3)
            scale_w0(0)
            scale_w0(1)
            for t in range(4):
                keep_mixed(t, t % 2)
                if t % 2:
                    scale_w0(2 + t // 2)
            act.wait_ge(taps_split, 4)
            for r in range(4):
                keep_mixed(2 * r + 4, 0)
                keep_mixed(2 * r + 5, 1)
                scale_w0(r + 4)
                act.wait_ge(ld_f1[0 if r < 2 else r], 16)
                cast_w1(r)
            for m in range(KT):
                act.wait_ge(w0q, m + 1)
                keep_mixed(m + 12, m % 2)
                keep_turned(m % 4, f0T[:, :, m * P:(m + 1) * P], bf16, m)
                if m % 2:
                    n = 4 + m // 2
                    act.wait_ge(ld_f1[n], 16)
                    cast_w1(n)
            act.wait_ge(w1_cast, KT)
            with act.Fori(0, KT - 3, 4) as i:
                for m in range(4):
                    keep_mixed(i + m + 20, m % 2)
                    keep_turned(m, f1T[:, :, bass.ds((i + m) * P, P)], fp16, i + m + KT)
            for t in range(T - 4, T):
                keep_mixed(t, t % 2)

            def scaled(t):
                nc.scalar.activation(slot_dyn(t + 2), slot_dyn(t + 2), ACT.Copy, scale=x_mul).then_inc(v_done, 1)

            def hi(t):
                v = slot_dyn(t).rearrange("p (s r) -> p r s", r=R8)
                act.wait_ge(pads, 1)
                for h in range(2):
                    act.wait_ge(x1_done, 2 * t + h + 1)
                    if h == 0:
                        act.wait_ge(split_out, 16 * t)
                    r = slice(4 * h, 4 * h + 4)
                    s0 = h
                    nc.scalar.copy(split[:, r, s0:s0 + S, 0], v[:, r, :]).then_inc(hi_done, 1)

            def yhi(t, n):
                for b in range(NB):
                    act.wait_ge(y1_done, 2 * t + b + 1)
                    nc.scalar.copy(y1s[n][:, 0, :, b * C:(b + 1) * C], y1[:, b, :, :]).then_inc(yhi_done, 1)

            act.wait_ge(x_step, 4)
            scaled(0)
            scaled(1)
            act.wait_ge(pads, 1)
            v0 = slot(0).rearrange("p (s r) -> p r s", r=R8)
            for h in range(2):
                act.wait_ge(x1_done, h + 1)
                r = slice(4 * h, 4 * h + 4)
                nc.scalar.copy(split[:, r, h:h + S, 0], v0[:, r, :]).then_inc(hi_done, 1)
            scaled(2)
            hi(1)
            yhi(0, 0)
            with act.Fori(2, T - 2 - 1, 2) as i:
                for n in range(2):
                    scaled(i + n + 1)
                    hi(i + n)
                    yhi(i + n - 1, 1 - n)
            scaled(T - 1)
            hi(T - 2)
            yhi(T - 3, 1)
            hi(T - 1)
            yhi(T - 2, 0)
            yhi(T - 1, 1)

        def round_e4m3(dve, src, z, dst, step, n0, done):
            nc.vector.tensor_scalar(z.bitcast(i32), src.bitcast(i32), 0x7F800000, 0x00400000,
                                    ALU.bitwise_and, ALU.bitwise_or).then_inc(step, 1)
            dve.wait_ge(step, n0 + 1)
            nc.vector.tensor_scalar(z, z, 1.5 * 2.0 ** -6, FP8_STEP, ALU.max, ALU.mult).then_inc(step, 1)
            dve.wait_ge(step, n0 + 2)
            nc.vector.tensor_tensor(src, src, z, ALU.add).then_inc(step, 1)
            dve.wait_ge(step, n0 + 3)
            nc.vector.tensor_tensor(dst, src, z, ALU.subtract).then_inc(done, 1)

        @block.vector
        def _(dve):
            dve.wait_ge(mlp_mm, 5)
            nc.vector.tensor_reduce(nmax, ps[3][0:B, 0:K], AX.X, ALU.max, negate=True).then_inc(mlp_ev, 1)
            dve.wait_ge(mlp_ev, 6)
            nc.vector.reciprocal(rinv, rsum).then_inc(mlp_ev, 1)
            dve.wait_ge(mlp_ev, 7)
            nc.vector.tensor_scalar(att, ex, rinv, None, ALU.mult).then_inc(mlp_ev, 1)

            def scales(vmax, inv, mul, src, step, n0):
                nc.vector.tensor_scalar(vmax, src, 1e-12, None, ALU.max).then_inc(step, 1)
                dve.wait_ge(step, n0 + 1)
                nc.vector.tensor_scalar(inv, vmax, 1.0 / FP8_MAX, None, ALU.mult).then_inc(step, 1)
                dve.wait_ge(step, n0 + 2)
                nc.vector.reciprocal(mul, inv).then_inc(step, 1)
                dve.wait_ge(step, n0 + 3)

            dve.wait_ge(mlp_ev, 10)
            nc.vector.tensor_copy(mixp[:, 0, :], mixb).then_inc(bias_parts, 1)
            dve.wait_ge(bias_parts, 1)
            nc.vector.tensor_tensor(mixr, mixb, mixp[:, 0, :], ALU.subtract).then_inc(bias_parts, 1)
            dve.wait_ge(bias_parts, 2)
            nc.vector.tensor_copy(mixp[:, 1, :], mixr).then_inc(bias_parts, 1)
            dve.wait_ge(bias_parts, 3)
            nc.vector.tensor_tensor(mixp[:, 2, :], mixr, mixp[:, 1, :], ALU.subtract).then_inc(bias_parts, 1)
            for h, name in enumerate(("f0a", "f0b")):
                dve.wait_ge(ld[name], 16)
                nc.vector.tensor_reduce(w_half[:, h:h + 1], w0f[:, 4 * h:4 * h + 4, :].rearrange("p r l -> p (r l)"),
                                        AX.X, ALU.max, apply_absolute_value=True).then_inc(w_red, 1)
            dve.wait_ge(w_red, 2)
            nc.vector.tensor_tensor(w_part, w_half[:, 0:1], w_half[:, 1:2], ALU.max).then_inc(w_red, 1)
            dve.wait_ge(zeroed, 5)
            for q in range(4):
                dve.wait_ge(mix_mm, q + 1)
                for b in range(NB):
                    ev = nc.vector.tensor_copy(mix_dst(q, 1, b), mix_src(q, 1, b))
                ev.then_inc(mix_odd, 1)
            dve.wait_ge(w_pe, 1)
            nc.vector.tensor_reduce(w_all, ps[7][0:1, 0:P], AX.X, ALU.max).then_inc(w_red, 1)
            dve.wait_ge(w_pe, 2)
            scales(w_max, w_inv, w_mul, ps[7][:, 128:129], w_step, 0)
            for r in range(R8):
                if r == 1:
                    dve.wait_ge(ld["taps"], 16 * R8)
                    tv = tapsf.rearrange("p o (h r) -> p h o r", h=2)
                    for h in range(2):
                        nc.vector.tensor_copy(taps16[:, 0, h, :, :], tv[:, h]).then_inc(taps_split, 1)
                    dve.wait_ge(taps_split, 2)
                    for h in range(2):
                        nc.vector.tensor_tensor(taps16[:, 1, h, :, :], tv[:, h], taps16[:, 0, h, :, :], ALU.subtract)\
                            .then_inc(taps_split, 1)
                if r:
                    dve.wait_ge(w0q, r)
                dve.wait_ge(w0v, r + 1)
                round_e4m3(dve, w0f[:, r, :], wz, w0c[:, r, :], w_chain, 3 * r, w0q)

            with dve.Fori(0, T, 1) as i:
                dve.wait_ge(mixed_ev, 2 * i + 2)
                nc.vector.tensor_reduce(stat[:, bass.ds(i, 1)], slot_dyn(i + 2), AX.X, ALU.max,
                                        apply_absolute_value=True).then_inc(mixed_red, 1)
            dve.wait_ge(mixed_red, T)
            nc.vector.tensor_reduce(part_max, amax_t, AX.X, ALU.max).then_inc(mixed_red, 1)
            dve.wait_ge(x_pe, 1)
            nc.vector.tensor_reduce(x_all, ps[7][0:1, 0:P], AX.X, ALU.max).then_inc(mixed_red, 1)
            dve.wait_ge(x_pe, 2)
            scales(x_max, x_inv, x_mul, ps[7][:, 128:129], x_step, 0)
            nc.vector.tensor_tensor(acc_mul, x_inv, w_inv, ALU.mult).then_inc(x_step, 1)
            dve.wait_ge(x_step, 4)

            def quantise(t, n):
                if not (isinstance(t, int) and t == 0):
                    dve.wait_ge(q_done, t)
                dve.wait_ge(v_done, t + 1)
                round_e4m3(dve, slot_dyn(t + 2), qz, qT[n].rearrange("p k m -> p (k m)"), q_step, 3 * t, q_done)

            def residual0(t):
                v = slot_dyn(t).rearrange("p (s r) -> p r s", r=R8)
                dve.wait_ge(xb_done, t + 1)
                for h in range(2):
                    dve.wait_ge(f0_done, 2 * t + h + 1)
                    r = slice(4 * h, 4 * h + 4)
                    nc.vector.scalar_tensor_tensor(out=v[:, r, :], in0=ps[h][:, :].rearrange("p (r s) -> p r s", r=4),
                                                   scalar=acc_mul, in1=v[:, r, :], op0=ALU.mult, op1=ALU.add)\
                        .then_inc(x1_done, 1)

            def lo(t):
                v = slot_dyn(t).rearrange("p (s r) -> p r s", r=R8)
                for h in range(2):
                    dve.wait_ge(hi_done, 2 * t + h + 1)
                    r = slice(4 * h, 4 * h + 4)
                    s = slice(h, h + S)
                    nc.vector.tensor_tensor(split[:, r, s, 1], v[:, r, :], split[:, r, s, 0], ALU.subtract)\
                        .then_inc(lo_done, 1)

            def add_ctx(t, n, ge, first=False):
                dve.wait_ge(ld_ctx[n], ge)
                for b in range(NB):
                    dve.wait_ge(conv_done, 2 * t + b + 1)
                    if not first:
                        dve.wait_ge(yhi_done, 2 * t - 1 + b)
                        dve.wait_ge(ylo_done, 2 * t - 1 + b)
                    nc.vector.tensor_tensor(y1[:, b, :, :], ps[4 + b][:, :].rearrange("p (m r) -> p r m", r=R8),
                                            rowvec[:, n, b * C:(b + 1) * C].unsqueeze(1).to_broadcast([P, R8, C]),
                                            ALU.add).then_inc(y1_done, 1)

            def ylo(t, n):
                for b in range(NB):
                    dve.wait_ge(yhi_done, 2 * t + b + 1)
                    nc.vector.tensor_tensor(y1s[n][:, 1, :, b * C:(b + 1) * C], y1[:, b, :, :],
                                            y1s[n][:, 0, :, b * C:(b + 1) * C], ALU.subtract).then_inc(ylo_done, 1)

            def residual1(t, h):
                dve.wait_ge(x1b_done, t + 1)
                dve.wait_ge(f1_done, 2 * t + h + 1)
                v = Y[:, bass.ds(t * L + h * H, H)]
                nc.vector.tensor_tensor(v, ps[2 + h][:, :], v, ALU.add).then_inc(res_done, 1)

            quantise(0, 0)
            residual0(0)
            lo(0)
            quantise(1, 1)
            residual0(1)
            lo(1)
            quantise(2, 0)
            add_ctx(0, 0, 16, True)
            ylo(0, 0)

            def step(t, n, ctx_ge, more=True):
                residual0(t)
                lo(t)
                if more:
                    quantise(t + 1, 1 - n)
                residual1(t - 2, 0)
                add_ctx(t - 1, 1 - n, ctx_ge)
                ylo(t - 1, 1 - n)
                residual1(t - 2, 1)

            with dve.Fori(2, T - 2 - 1, 2) as i:
                step(i, 0, 8 * i)
                step(i + 1, 1, 8 * i + 16)
            step(T - 2, 0, 8 * (T - 2))
            step(T - 1, 1, 8 * (T - 2) + 16, False)
            residual1(T - 2, 0)
            add_ctx(T - 1, 1, 8 * T)
            ylo(T - 1, 1)
            residual1(T - 2, 1)
            residual1(T - 1, 0)
            residual1(T - 1, 1)

        @block.tensor
        def _(pe):
            mm = nc.tensor.matmul
            pe.wait_ge(ident_made, 1)
            pe.wait_ge(ld["mlp"], 160)
            nc.tensor.transpose(ps[0][:, 0:B], emb, ident[0:B, 0:B]).then_inc(mlp_mm, 1)
            nc.tensor.transpose(ps[7][:, 0:C], ctw, ident[0:C, 0:C]).then_inc(mlp_mm, 1)
            pe.wait_ge(mlp_ev, 1)
            mm(ps[1][:, 0:B], mw0, embT, start=True, stop=True).then_inc(mlp_mm, 1)
            pe.wait_ge(mlp_ev, 3)
            mm(ps[2][:, 0:B], mw1, h0T, start=True, stop=True).then_inc(mlp_mm, 1)
            pe.wait_ge(mlp_ev, 4)
            mm(ps[3][0:B, 0:K], h1T, mw2, start=True, stop=False)
            mm(ps[3][0:B, 0:K], ones[0:1, 0:B], rowb, start=False, stop=True).then_inc(mlp_mm, 1)
            pe.wait_ge(mlp_ev, 8)
            nc.tensor.transpose(ps[4][0:K, 0:B], att, ident[0:B, 0:B]).then_inc(mlp_mm, 1)
            pe.wait_ge(mlp_ev, 9)
            mm(ps[5][0:B, 0:C], attT, mbk, start=True, stop=True).then_inc(mlp_mm, 1)
            mm(ps[6][0:B, 0:C], embT, ctwT, start=True, stop=False)
            mm(ps[6][0:B, 0:C], ones[0:1, 0:B], rowf, start=False, stop=True).then_inc(mlp_mm, 1)
            pe.wait_ge(ld["wk"], 16)
            for q in range(4):
                for j in range(8):
                    o2 = 2 * (8 * q + j)
                    last = mm(ps[q][:, j * B:(j + 1) * B], wk[:, o2:o2 + 2, :].rearrange("k o i -> k (o i)"),
                              attT, start=True, stop=True)
                last.then_inc(mix_mm, 1)
            pe.wait_ge(mlp_ev, N_MLP)
            pe.wait_ge(w_red, 3)
            nc.tensor.transpose(ps[7][0:1, 0:P], w_part, ident[:, :]).then_inc(w_pe, 1)
            pe.wait_ge(w_red, 4)
            mm(ps[7][:, 128:129], ones, w_all, start=True, stop=True).then_inc(w_pe, 1)
            pe.wait_ge(mix_even, 4)
            pe.wait_ge(mix_odd, 4)
            pe.wait_ge(zeroed, 5)

            def mixed_tile(t, n, ge, first=False):
                m = n % 2
                pe.wait_ge(ld_x[n], ge)
                pe.wait_ge(ld_rb[n], ge)
                for h in range(2):
                    if not first:
                        pe.wait_ge(mixed_ev, 2 * t + h - 3)
                    mm(ps[2 * m + h][:, :].rearrange("p (k m) -> p k m", m=P), ones_b,
                       rowb3[:, n, :].unsqueeze(1).to_broadcast([3, H // P, P]), start=True, stop=False,
                       skip_group_check=True)
                    for k in range(4):
                        j = 4 * h + k
                        last = mm(ps[2 * m + h][:, k * P:(k + 1) * P], xring[n][:, j * P:(j + 1) * P],
                                  mixw_dyn(t), start=False, stop=(k == 3), skip_group_check=True)
                    last.then_inc(mixed, 1)

            def turned(m, dt, src, idt, at, ready, ge):
                pe.wait_ge(ready, ge)
                if at is not None:
                    pe.wait_ge(wT_ev, at)
                pb = ps[4 + m][:, :].bitcast(dt)
                for k in range(KT):
                    last = nc.tensor.transpose(pb[:, k * P:(k + 1) * P], src(k), idt)
                last.then_inc(wT_mm, 1)

            def turned0(r, m, at):
                turned(m, bf16, lambda k: w0c_dyn(r, k), ident_b, at, w0q, r + 1)

            def turned1(n, m, at):
                turned(m, fp16, lambda k: w1c_dyn(n, k), ident_h, at, w1d, n + 1)

            for n in range(4):
                mixed_tile(n, n, 16, n < 2)
            with pe.Fori(4, 12 - 3, 4) as i:
                for n in range(4):
                    mixed_tile(i + n, n, 4 * i + 16)
            pe.wait_ge(ident_cast, 2)
            pe.wait_ge(w_step, 3)
            for n in range(4):
                mixed_tile(12 + n, n, 64)
                turned0(n, n, None)
            for n in range(4):
                mixed_tile(16 + n, n, 80)
                turned0(4 + n, n, n + 1)
            with pe.Fori(0, KT - 3, 4) as i:
                for n in range(4):
                    mixed_tile(i + n + 20, n, 4 * i + 96)
                    turned1(i + n, n, i + n + 5)
            for n in range(4):
                mixed_tile(28 + n, n, 128)
            pe.wait_ge(mixed_red, T + 1)
            pe.wait_ge(wT_ev, 2 * KT)
            nc.tensor.transpose(ps[7][0:1, 0:P], part_max, ident[:, :]).then_inc(x_pe, 1)
            pe.wait_ge(mixed_red, T + 2)
            mm(ps[7][:, 128:129], ones, x_all, start=True, stop=True).then_inc(x_pe, 1)
            pe.wait_ge(taps_split, 4)

            def ffn0(t, n, first=False):
                pe.wait_ge(q_done, t + 1)
                for h in range(2):
                    if not first:
                        pe.wait_ge(x1_done, 2 * t - 1 + h)
                    for k in range(KT):
                        last = mm(ps[h][:, :], qT[n][:, k, :], f0T[:, k, h * H:(h + 1) * H],
                                  start=(k == 0), stop=(k == KT - 1))
                    last.then_inc(f0_done, 1)

            def conv(t, first=False):
                pe.wait_ge(split_in, 16 * t + 16)
                for b in range(NB):
                    if not first:
                        pe.wait_ge(y1_done, 2 * t - 1 + b)
                    for g in range(G):
                        parts = [(xp, wp, h) for xp, wp in ((0, 0), (0, 1), (1, 0)) for h in range(2)]
                        for j, (xp, wp, h) in enumerate(parts):
                            last = mm(ps[4 + b][:, g * P:(g + 1) * P], convin[:, b * G + g, h:h + S, xp],
                                      taps16[:, wp, h, g * CG:(g + 1) * CG, :].rearrange("p a b -> p (a b)"),
                                      start=(j == 0), stop=(j == len(parts) - 1))
                    last.then_inc(conv_done, 1)

            def ffn1(t, n, h, first=False):
                pe.wait_ge(ylo_done, 2 * t + 2)
                if not first:
                    pe.wait_ge(res_done, 2 * t - 1 + h)
                for e in range(2):
                    for k in range(KT):
                        last = mm(ps[2 + h][:, :], y1s[n][:, e, k, :], f1T[:, k, h * H:(h + 1) * H],
                                  start=(e == 0 and k == 0), stop=(e == 1 and k == KT - 1))
                last.then_inc(f1_done, 1)

            ffn0(0, 0, True)
            ffn0(1, 1)
            conv(0, True)

            def step(t, n, first=False):
                ffn0(t, n)
                ffn1(t - 2, n, 0, first)
                conv(t - 1)
                ffn1(t - 2, n, 1, first)

            step(2, 0, True)
            step(3, 1)
            with pe.Fori(4, T - 1, 2) as i:
                step(i, 0)
                step(i + 1, 1)
            ffn1(T - 2, 0, 0)
            conv(T - 1)
            ffn1(T - 2, 0, 1)
            ffn1(T - 1, 1, 0)
            ffn1(T - 1, 1, 1)



_INS = ['x', 'cond_128', 'fside_S_0', 'L0_cond_W0', 'L0_cond_b0', 'L0_cond_W1', 'L0_cond_b1', 'L0_cond_W2',
        'L0_cond_b2', 'L0_cond_weight', 'L0_cond_bias_k', 'L0_ffn_weight', 'L0_ffn_bias', 'L1_cond_weight',
        'L1_cond_c_weight', 'L1_ffn_W_q', 'L1_ffn_scale', 'L1_ffn_zero', 'L1_ffn_bias']


def kernel(**inputs):
    import numpy as _np
    import concourse.bacc as _bacc
    from concourse import mybir as _mybir
    from concourse.bass_utils import run_bass_kernel_spmd as _run

    nc = _bacc.Bacc("TRN2", target_bir_lowering=False, num_devices=1)
    arrays, args = {}, []
    for name in _INS:
        a = _np.ascontiguousarray(inputs[name])
        arrays[f"in_{name}_dram"] = a
        args.append(nc.dram_tensor(f"in_{name}_dram", a.shape, _mybir.dt.from_np(a.dtype), kind="ExternalInput").ap())
    out = nc.dram_tensor("out_dram", inputs['x'].shape, _mybir.dt.float32, kind="ExternalOutput").ap()
    adaln_ffn_kernel(nc, *args, out)
    return _run(nc, [arrays], core_ids=[0]).results[0]["out_dram"]
```

```python
import concourse.bass as bass
from concourse import mybir
from contextlib import ExitStack


def adaln_ffn_kernel(nc, x, cond, fside, cw0, cb0, cw1, cb1, cw2, cb2, cwk, cbk,
                     f0w, f0b, convw, ctxw, f1q, f1s, f1z, f1b, out):
    fp32, bf16, fp16, i32 = mybir.dt.float32, mybir.dt.bfloat16, mybir.dt.float16, mybir.dt.int32
    ALU, ACT, AX = mybir.AluOpType, mybir.ActivationFunctionType, mybir.AxisListType

    B, C, L = x.shape
    P = 128
    T = B * C // P
    NB = P // C
    K = cwk.shape[0]
    D = cond.shape[1]
    CG, TAPS = convw.shape[1], convw.shape[2]
    G = C // CG
    R8 = P // CG
    S = L // R8
    PAD = TAPS // 2
    KT = L // P
    NG = f1s.shape[1]
    H = 512
    BG = NB * G
    SW = S + 2
    FP8_MAX, FP8_STEP = 448.0, 2.0 ** 20
    assert (T, KT, R8, S, BG, D, L) == (32, 8, 8, 128, 8, P, 2 * H)

    x_t = x.rearrange("(t b) c l -> t (b c) l", b=NB)
    out_t = out.rearrange("(t b) c l -> t (b c) l", b=NB)

    ctx = ExitStack()
    with ctx:
        def sb(name, shape, dt):
            return ctx.enter_context(nc.sbuf_tensor(name, shape, dt))

        def sem(name):
            return ctx.enter_context(nc.semaphore(name))

        row_bias_d = nc.dram_tensor("row_bias", (3, T, P), bf16, kind="Internal").ap()
        row_ctx_d = nc.dram_tensor("row_ctx", (T, P), fp32, kind="Internal").ap()
        wkp_d = nc.dram_tensor("mixing_kernel_parts", (3, 3, K, C * C), bf16, kind="Internal").ap()
        split_d = nc.dram_tensor("split_rows", (2, P, R8 * SW * 2), fp16, kind="Internal").ap()

        Y = sb("Y", [P, (T + 2) * L], fp32)
        f0T = sb("f0T", [P, KT, L], bf16)
        f1T = sb("f1T", [P, KT, L], fp16)
        work = sb("work", [P, 7200], fp32)
        bias0 = sb("bias0", [P, L], fp32)
        bias1 = sb("bias1", [P, L], fp16)
        taps16 = sb("taps16", [P, 2, 2, C, R8], fp16)
        rowvec = sb("rowvec", [P, 2, P], fp32)
        ident = sb("ident", [P, P], fp32)
        stat = sb("stat", [P, 48], fp32)

        def slot(n, k=1):
            return Y[:, n * L:(n + k) * L]

        def slot_dyn(t):
            return Y[:, bass.ds(t * L, L)]

        def mix_src(q, par, b):
            return ps[q][par * C:(par + 1) * C, :].rearrange("p (j t b) -> p b t j", t=T, b=NB)[:, b]

        def mix_dst(q, par, b):
            o = b * C + 16 * q + par
            return mixw[b * C:(b + 1) * C, :, o:o + 15:2]

        def held(eng, value):
            return value if isinstance(value, int) else eng.snap(value)

        def w0c_dyn(r, k):
            return f1T[:, r, k * P:(k + 1) * P].bitcast(bf16)

        def w1c_dyn(n, k):
            base = Y[:, W1C_SLOT * L:(W1C_SLOT + 4) * L].bitcast(fp16)
            return base[:, bass.ds(n * L + R8 - 1 - k, S, R8)]

        def mixw_dyn(t):
            return work[:, bass.ds(t * P, P)]

        mixw = work[:, 0:T * P].rearrange("p (t m) -> p t m", t=T)
        xring = [slot(0), slot(1), work[:, T * P:T * P + L], work[:, T * P + L:T * P + 2 * L]]
        KP = 9 * K
        wkp9 = Y[0:KP, 3 * L:5 * L].bitcast(bf16)
        KC = P // K
        KF = C * C // KC
        wkf, wkr = slot(5)[:, 0:KF], slot(5)[:, KF:2 * KF]
        wkp = Y[:, 5 * L + 2 * KF:6 * L].bitcast(bf16)[:, 0:3 * KF].rearrange("p (e f) -> p e f", e=3)
        attp = Y[0:B, 6 * L:6 * L + 64].bitcast(bf16)[:, 0:KP].rearrange("p (j i k) -> p j i k", j=3, i=3)
        attr = Y[0:B, 6 * L + 64:6 * L + 64 + K]
        attpT = Y[0:KP, 6 * L + 128:6 * L + 160].bitcast(bf16)
        tapsf = slot(13).rearrange("p (o w) -> p o w", w=2 * R8)
        mlp = slot(9)
        W0_SLOT, W1_SLOT, W1C_SLOT = 20, 28, 30
        w0f = slot(W0_SLOT, 8).rearrange("p (r l) -> p r l", r=R8)
        w1i = slot(W1_SLOT, 2).bitcast(i32).rearrange("p (n l) -> p n l", n=2)
        w1c = slot(W1C_SLOT, 4).bitcast(fp16).rearrange("p (n l) -> p n l", n=KT)
        w0c = f1T[:, :, :].bitcast(bf16)
        wz = [bias0[:, :], slot(33)]
        mw0, mw1 = mlp[:, 0:128], mlp[:, 128:256]
        emb, ctw = mlp[0:B, 256:384], mlp[0:C, 384:512]
        embT, ctwT = mlp[:, 512:576], mlp[:, 576:640]
        h0T, h1T = mlp[:, 640:704], mlp[:, 704:768]
        mw2 = mlp[:, 768:776]
        att = mlp[0:B, 776:784]
        attT = mlp[0:K, 784:848]
        mbk = mlp[0:K, 848:912]
        rowb = mlp[0:1, 912:920]
        rowf = mlp[0:1, 920:984]
        mb0, mb1 = mlp[:, 984:985], mlp[:, 985:986]
        ex = mlp[0:B, 986:994]
        mixb = work[0:B, 7000:7064]
        mixr = work[0:B, 6936:7000]
        mixp = work[0:B, 6600:6696].bitcast(bf16).rearrange("p (e o) -> p e o", e=3)
        mixc = work[0:B, 7064:7128]
        zs = bias1[:, 7 * P:8 * P]
        zero16, scale16 = zs[:, 0:KT * NG].rearrange("p (n g) -> p n g", g=NG), \
            zs[:, KT * NG:2 * KT * NG].rearrange("p (n g) -> p n g", g=NG)

        qz = work[:, 0:L]
        qT = [work[:, L + n * H:L + (n + 1) * H].bitcast(bf16).rearrange("p (k m) -> p k m", k=KT) for n in range(2)]
        o = 2 * L
        split = work[:, o:o + R8 * SW].bitcast(fp16).rearrange("p (r s e) -> p r s e", r=R8, e=2)
        o += R8 * SW
        convin = work[:, o:o + BG * SW].bitcast(fp16).rearrange("p (g s e) -> p g s e", g=BG, e=2)
        o += BG * SW
        y1 = work[:, o:o + L].rearrange("p (b r m) -> p b r m", b=NB, r=R8)
        o += L
        y1s = [work[:, o + n * L:o + (n + 1) * L].bitcast(fp16).rearrange("p (e k m) -> p e k m", e=2, k=KT)
               for n in range(2)]
        assert o + 2 * L <= 7200

        amax_t = stat[:, 0:T + 1]
        part_max, w_part = stat[:, 40:41], stat[:, 33:34]
        w_quarter = stat[:, 28:32]
        x_max, w_max = stat[:, 34:35], stat[:, 35:36]
        x_inv, w_inv = stat[:, 36:37], stat[:, 37:38]
        x_mul, w_mul = stat[:, 38:39], stat[:, 39:40]
        acc_mul = stat[:, 42:43]
        nmax, rsum, rinv = stat[0:B, 43:44], stat[0:B, 44:45], stat[0:B, 45:46]
        gelu_probe = stat[:, 41:42]
        w_all, x_all = stat[0:1, 46:47], stat[0:1, 47:48]

        ones = work[0:1, 6400:6400 + P]
        ident_b = bias1[:, 0:P].bitcast(bf16)
        ident_h = bias1[:, P:2 * P]
        ones_b = bias1[0:3, 2 * P:3 * P].bitcast(bf16)
        rowb3 = bias1[0:3, 3 * P:7 * P].bitcast(bf16).rearrange("p (n m) -> p n m", n=4)

        ps = [ctx.enter_context(nc.psum_tensor(f"ps{n}", [P, H], fp32)) for n in range(8)]

        ld = {n: sem("ld_" + n) for n in ("mlp", "wk", "wkp", "f0_0", "f0_1", "f0_2", "f0_3", "zs", "taps", "b0", "b1")}
        ld_f1 = [sem(f"ld_f1_{n}") for n in range(2)]
        ld_x = [sem(f"ld_x{n}") for n in range(4)]
        ld_rb = [sem(f"ld_rb{n}") for n in range(4)]
        zeroed = sem("zeroed")
        ident_made = sem("ident_made")
        ident_cast = sem("ident_cast")
        mlp_mm = sem("mlp_mm")
        mlp_ev = sem("mlp_ev")
        wk_parts = sem("wk_parts")
        wk_out = sem("wk_out")
        att_parts = sem("att_parts")
        attp_mm = sem("attp_mm")
        attp_ev = sem("attp_ev")
        mix_mm = sem("mix_mm")
        mix_even = sem("mix_even")
        mix_odd = sem("mix_odd")
        bias_parts = sem("bias_parts")
        w1_cast = sem("w1_cast")
        w1_step = sem("w1_step")
        rows_out = sem("rows_out")
        taps_split = sem("taps_split")
        w_red = sem("w_red")
        w_chain = sem("w_chain")
        w_pe = sem("w_pe")
        w_step = sem("w_step")
        w0v = sem("w0v")
        w0q = [sem("w0q_even"), sem("w0q_odd")]
        w1d = sem("w1d")
        wT_mm = sem("wT_mm")
        wT_ev = sem("wT_ev")
        mixed = sem("mixed")
        mixed_ev = sem("mixed_ev")
        mixed_red = sem("mixed_red")
        x_pe = sem("x_pe")
        x_step = sem("x_step")
        ld_x2 = [sem(f"ld_x2_{n}") for n in range(2)]
        ld_ctx = [sem(f"ld_ctx{n}") for n in range(2)]
        pads = sem("pads")
        xb_done = sem("xb_done")
        v_done = sem("v_done")
        q_step = sem("q_step")
        q_done = sem("q_done")
        f0_done = sem("f0_done")
        x1_done = sem("x1_done")
        hi_done = sem("hi_done")
        lo_done = sem("lo_done")
        x1b_done = sem("x1b_done")
        split_out = sem("split_out")
        split_in = sem("split_in")
        conv_done = sem("conv_done")
        y1_done = sem("y1_done")
        yhi_done = sem("yhi_done")
        ylo_done = sem("ylo_done")
        f1_done = sem("f1_done")
        res_done = sem("res_done")
        stored = sem("stored")

        block = ctx.enter_context(nc.Block())

        N_MLP = 11

        @block.sync
        def _(sp):
            col = lambda a: a.rearrange("(p a) -> p a", a=1)
            row = lambda a: a.rearrange("(a n) -> a n", a=1)
            sp.dma_start(wkf, cwk.rearrange("k (c o) i a -> (k c) (o i a)", c=KC)).then_inc(ld["wk"], 16)
            for dst, src in ((emb, cond), (mw0, cw0), (mb0, col(cb0)), (mw1, cw1), (mb1, col(cb1)), (mw2, cw2),
                             (rowb, row(cb2)), (mbk, cbk), (ctw, ctxw), (rowf, row(fside))):
                sp.dma_start(dst, src).then_inc(ld["mlp"], 16)
            f0_rows = f0w.rearrange("(s r) l -> s r l", r=R8)

            def load_f0(h):
                sp.dma_start(w0f[:, 2 * h:2 * h + 2, :], f0_rows[:, 2 * h:2 * h + 2, :]).then_inc(ld[f"f0_{h}"], 16)

            sp.wait_ge(wk_parts, 4)
            for i in range(3):
                sp.dma_start(wkp_d[:, i].rearrange("e k (c f) -> (k c) e f", c=KC), wkp).then_inc(wk_out, 16)
            sp.dma_start(xring[0], x_t[0]).then_inc(ld_x[0], 16)
            sp.dma_start(xring[1], x_t[1]).then_inc(ld_x[1], 16)
            sp.wait_ge(wk_out, 48)
            sp.dma_start(wkp9, wkp_d.rearrange("j i k f -> (j i k) f")).then_inc(ld["wkp"], 16)
            load_f0(0)
            sp.wait_ge(mlp_ev, N_MLP)
            sp.wait_ge(bias_parts, 4)
            sp.dma_start(row_bias_d.rearrange("e t (b o) -> (t b) e o", b=NB), mixp).then_inc(rows_out, 16)
            sp.dma_start(row_ctx_d.rearrange("t (b o) -> (t b) o", b=NB), mixc).then_inc(rows_out, 16)
            sp.dma_start(xring[2], x_t[2]).then_inc(ld_x[2], 16)
            sp.dma_start(xring[3], x_t[3]).then_inc(ld_x[3], 16)
            sp.wait_ge(rows_out, 32)
            for n in range(4):
                sp.dma_start(rowb3[:, n, :], row_bias_d[:, n, :]).then_inc(ld_rb[n], 16)
            load_f0(1)

            def settled():
                sp.wait_ge(rows_out, 32)

            def next_tile(t, n):
                settled()
                sp.wait_ge(mixed, 2 * t + 2)
                sp.dma_start(rowb3[:, n, :], row_bias_d[:, bass.ds(t + 4, 1), :]).then_inc(ld_rb[n], 16)
                sp.dma_start(xring[n], x_t[t + 4]).then_inc(ld_x[n], 16)

            def load_f1(row, n):
                sp.dma_start(w1i[:, n, :], f1q[bass.ds(row, P), :]).then_inc(ld_f1[n], 16)

            for t in range(12):
                next_tile(t, t % 4)
                if t in (2, 4):
                    load_f0(t // 2 + 1)
                if t == 6:
                    sp.dma_start(zero16, f1z.rearrange("(n p) g -> p n g", p=P)).then_inc(ld["zs"], 16)
                    sp.dma_start(scale16, f1s.rearrange("(n p) g -> p n g", p=P)).then_inc(ld["zs"], 16)
                if t in (6, 8):
                    load_f1((t // 2 - 3) * P, t // 2 - 3)
            with sp.Fori(0, (KT - 2) // 2, 1) as i:
                for n in range(4):
                    next_tile(4 * i + 12 + n, n)
                    if n % 2 == 0:
                        settled()
                        sp.wait_ge(w1_cast, 2 * i + 1 + n // 2)
                        load_f1(2 * P * i + (2 + n // 2) * P, n // 2)
            for t in range(24, T - 4):
                next_tile(t, t % 4)

            def load_x(t, n):
                sp.dma_start(slot_dyn(t), x_t[t]).then_inc(ld_x2[n], 16)

            def load_ctx(t, n):
                sp.dma_start(rowvec[:, n, :], row_ctx_d[bass.ds(t, 1), :].to_broadcast([P, P]))\
                    .then_inc(ld_ctx[n], 16)

            def store(t):
                settled()
                sp.wait_ge(res_done, 2 * t + 2)
                sp.dma_start(out_t[t], slot_dyn(t)).then_inc(stored, 16)

            def turn(t, n, conv_read):
                both, back = held(sp, 2 * t + 2), held(sp, 16 * t + 16)
                if conv_read is not None:
                    conv_read = held(sp, conv_read)
                sp.wait_ge(lo_done, both)
                sp.dma_start(split_d[n], split.rearrange("p r s e -> p (r s e)")).then_inc(split_out, 16)
                sp.wait_ge(split_out, back)
                if conv_read is not None:
                    sp.wait_ge(conv_done, conv_read)
                sp.dma_start(convin.rearrange("p g s e -> p g (s e)"),
                             split_d[n].rearrange("(g c) (r f) -> (c r) g f", g=BG, r=R8)).then_inc(split_in, 16)

            load_ctx(0, 0)
            load_ctx(1, 1)
            sp.wait_ge(w0q[0], R8 // 2)
            sp.dma_start(bias0[:, :], row(f0b).to_broadcast([P, L])).then_inc(ld["b0"], 16)
            sp.wait_ge(mixed, 2 * T)
            load_x(0, 0)
            load_x(1, 1)
            sp.wait_ge(w1d, KT)
            sp.dma_start(bias1[:, :], row(f1b).to_broadcast([P, L])).then_inc(ld["b1"], 16)
            for t in range(2):
                sp.wait_ge(q_done, t + 1)
                sp.wait_ge(xb_done, t + 1)
                load_x(t + 2, t)
                turn(t, t, 2 * t if t else None)

            def phase2(t, n, more):
                if more:
                    settled()
                    sp.wait_ge(q_done, t + 1)
                    sp.wait_ge(xb_done, t + 1)
                    load_x(t + 2, n)
                settled()
                sp.wait_ge(y1_done, 2 * t - 2)
                load_ctx(t, n)
                turn(t, n, 2 * t)
                store(t - 2)

            with sp.Fori(2, T - 2 - 1, 2) as i:
                for n in range(2):
                    phase2(i + n, n, True)
            for n in range(2):
                phase2(T - 2 + n, n, False)
            store(T - 2)
            for h in range(2):
                sp.wait_ge(res_done, 2 * T - 1 + h)
                sp.dma_start(out_t[T - 1, :, h * H:(h + 1) * H], slot(T - 1)[:, h * H:(h + 1) * H])\
                    .then_inc(stored, 16)
            sp.wait_ge(stored, 16 * (T + 1))

        @block.gpsimd
        def _(pool):
            nc.gpsimd.memset(ident[:, :], 0.0).then_inc(zeroed, 1)
            nc.gpsimd.memset(ones, 1.0).then_inc(zeroed, 1)
            pool.wait_ge(zeroed, 2)
            nc.gpsimd.affine_select(out=ident[:, :], in_=ident[:, :], compare_op=ALU.not_equal, fill=1.0, base=0,
                                    pattern=[[-1, P]], channel_multiplier=1).then_inc(ident_made, 1)
            nc.gpsimd.memset(tapsf, 0.0).then_inc(zeroed, 1)
            nc.gpsimd.memset(ones_b, 1.0).then_inc(zeroed, 1)
            pool.wait_ge(zeroed, 3)
            for r in range(R8):
                q = (r + PAD) % R8
                pool.dma_start(tapsf[r::R8, :, R8 - 1 - q:R8 - 1 - q + TAPS],
                               convw.rearrange("o c k -> c o k")).then_inc(ld["taps"], 16)
            nc.gpsimd.memset(mixw, 0.0).then_inc(zeroed, 1)
            grp = lambda a: a.rearrange("p (g k) -> p g k", g=NG)
            wide = lambda a: a.unsqueeze(2).to_broadcast([P, NG, L // NG])
            pool.wait_ge(ld["zs"], 32)
            for n in range(KT):
                if n < R8 // 2:
                    r = 2 * n
                    pool.wait_ge(w_chain, 3 * r + 3)
                    nc.gpsimd.tensor_tensor(w0c[:, r, :], w0f[:, r, :], wz[0], ALU.subtract).then_inc(w0q[0], 1)
                pool.wait_ge(w1_cast, n + 1)
                nc.gpsimd.tensor_tensor(grp(w1c[:, n, :]), grp(w1c[:, n, :]), wide(zero16[:, n, :]),
                                        ALU.subtract).then_inc(w1_step, 1)
                pool.wait_ge(w1_step, n + 1)
                nc.gpsimd.tensor_tensor(grp(w1c[:, n, :]), grp(w1c[:, n, :]), wide(scale16[:, n, :]),
                                        ALU.mult).then_inc(w1d, 1)
            pool.wait_ge(x_step, 4)
            nc.gpsimd.memset(split, 0.0).then_inc(pads, 1)

            def add_bias0(t, n, ge):
                pool.wait_ge(ld["b0"], 16)
                pool.wait_ge(ld_x2[n], ge)
                nc.gpsimd.tensor_tensor(slot_dyn(t), slot_dyn(t), bias0[:, :], ALU.add).then_inc(xb_done, 1)

            def add_bias1(t):
                parts = held(pool, 2 * t + 2)
                pool.wait_ge(ld["b1"], 16)
                pool.wait_ge(lo_done, parts)
                nc.gpsimd.tensor_tensor(slot_dyn(t), slot_dyn(t), bias1[:, :], ALU.add).then_inc(x1b_done, 1)

            add_bias0(0, 0, 16)
            add_bias0(1, 1, 16)
            with pool.Fori(0, T - 2 - 1, 2) as i:
                add_bias1(i)
                add_bias0(i + 2, 0, 8 * i + 32)
                add_bias1(i + 1)
                add_bias0(i + 3, 1, 8 * i + 32)
            add_bias1(T - 2)
            add_bias1(T - 1)

        @block.scalar
        def _(act):
            act.wait_ge(ident_made, 1)
            nc.scalar.copy(ident_b, ident[:, :]).then_inc(ident_cast, 1)
            nc.scalar.copy(ident_h, ident[:, :]).then_inc(ident_cast, 1)
            nc.scalar.activation(gelu_probe, ident[:, 0:1], ACT.Gelu).then_inc(ident_cast, 1)
            act.wait_ge(mlp_mm, 1)
            nc.scalar.copy(embT, ps[0][:, 0:B]).then_inc(mlp_ev, 1)
            act.wait_ge(mlp_mm, 2)
            nc.scalar.copy(ctwT, ps[7][:, 0:C]).then_inc(mlp_ev, 1)
            act.wait_ge(ld["mlp"], 160)
            act.wait_ge(mlp_mm, 3)
            nc.scalar.activation(h0T, ps[1][:, 0:B], ACT.Gelu, bias=mb0).then_inc(mlp_ev, 1)
            act.wait_ge(mlp_mm, 4)
            nc.scalar.activation(h1T, ps[2][:, 0:B], ACT.Gelu, bias=mb1).then_inc(mlp_ev, 1)
            act.wait_ge(mlp_ev, 5)
            nc.scalar.activation(ex, ps[3][0:B, 0:K], ACT.Exp, bias=nmax, accum_out=rsum).then_inc(mlp_ev, 1)
            act.wait_ge(mlp_mm, 6)
            nc.scalar.copy(attT, ps[4][0:K, 0:B]).then_inc(mlp_ev, 1)
            act.wait_ge(attp_mm, 1)
            nc.scalar.copy(attpT, ps[1][:, :].bitcast(bf16)[0:KP, 0:B]).then_inc(attp_ev, 1)
            act.wait_ge(mlp_mm, 7)
            nc.scalar.copy(mixb, ps[5][0:B, 0:C]).then_inc(mlp_ev, 1)
            act.wait_ge(mlp_mm, 8)
            nc.scalar.copy(mixc, ps[6][0:B, 0:C]).then_inc(mlp_ev, 1)
            act.wait_ge(zeroed, 5)
            for q in range(4):
                act.wait_ge(mix_mm, q + 1)
                for b in range(NB):
                    ev = nc.scalar.copy(mix_dst(q, 0, b), mix_src(q, 0, b))
                ev.then_inc(mix_even, 1)

            def keep_mixed(t, m):
                for h in range(2):
                    act.wait_ge(mixed, 2 * t + h + 1)
                    nc.scalar.copy(Y[:, bass.ds((t + 2) * L + h * H, H)], ps[2 * m + h][:, :]).then_inc(mixed_ev, 1)

            def keep_turned(m, dst, dt, at):
                act.wait_ge(wT_mm, at + 1)
                pb = ps[4 + m][:, :].bitcast(dt).rearrange("p (k q) -> p k q", k=KT)
                nc.scalar.copy(dst, pb).then_inc(wT_ev, 1)

            def scale_w0(r):
                wr = Y[:, bass.ds((r + W0_SLOT) * L, L)]
                nc.scalar.activation(wr, wr, ACT.Copy, scale=w_mul).then_inc(w0v, 1)

            def cast_w1(n):
                act.wait_ge(ld_f1[n % 2], 16 * (n // 2) + 16)
                nc.scalar.copy(w1c[:, n, :], w1i[:, n % 2, :]).then_inc(w1_cast, 1)

            with act.Fori(0, 10 - 1, 2) as i:
                for m in range(2):
                    keep_mixed(i + m, m)
            act.wait_ge(w_step, 3)
            scale_w0(0)
            keep_mixed(10, 0)
            scale_w0(1)
            act.wait_ge(taps_split, 4)
            for t in range(11, 16):
                keep_mixed(t, t % 2)
                scale_w0(t - 9)
                if t % 2:
                    cast_w1((t - 11) // 2)
            for r in range(R8):
                if r >= 2:
                    act.wait_ge(w0q[r % 2], r // 2)
                keep_mixed(16 + r, r % 2)
                if r == 0:
                    scale_w0(7)
                keep_turned(r % 4, f0T[:, :, r * P:(r + 1) * P], bf16, r)
                if r % 2:
                    cast_w1(3 + r // 2)
            for n in range(KT - 1):
                if n == 2:
                    act.wait_ge(w1_cast, KT)
                keep_mixed(24 + n, n % 2)
                keep_turned(n % 4, f1T[:, :, n * P:(n + 1) * P], fp16, KT + n)
                if n == 1:
                    cast_w1(7)
            keep_turned(3, f1T[:, :, 7 * P:8 * P], fp16, 2 * KT - 1)
            keep_mixed(T - 1, 1)

            def scaled(t):
                nc.scalar.activation(slot_dyn(t + 2), slot_dyn(t + 2), ACT.Copy, scale=x_mul).then_inc(v_done, 1)

            def hi(t):
                v = slot_dyn(t).rearrange("p (s r) -> p r s", r=R8)
                act.wait_ge(pads, 1)
                for h in range(2):
                    act.wait_ge(x1_done, 2 * t + h + 1)
                    if h == 0:
                        act.wait_ge(split_out, 16 * t)
                    r = slice(4 * h, 4 * h + 4)
                    s0 = h
                    nc.scalar.copy(split[:, r, s0:s0 + S, 0], v[:, r, :]).then_inc(hi_done, 1)

            def yhi(t, n):
                for b in range(NB):
                    act.wait_ge(y1_done, 2 * t + b + 1)
                    nc.scalar.copy(y1s[n][:, 0, :, b * C:(b + 1) * C], y1[:, b, :, :]).then_inc(yhi_done, 1)

            act.wait_ge(x_step, 3)
            scaled(1)
            scaled(2)
            act.wait_ge(pads, 1)
            v0 = slot(0).rearrange("p (s r) -> p r s", r=R8)
            for h in range(2):
                act.wait_ge(x1_done, h + 1)
                r = slice(4 * h, 4 * h + 4)
                nc.scalar.copy(split[:, r, h:h + S, 0], v0[:, r, :]).then_inc(hi_done, 1)
            hi(1)
            yhi(0, 0)
            with act.Fori(2, T - 2 - 1, 2) as i:
                for n in range(2):
                    scaled(i + n + 1)
                    hi(i + n)
                    yhi(i + n - 1, 1 - n)
            scaled(T - 1)
            hi(T - 2)
            yhi(T - 3, 1)
            hi(T - 1)
            yhi(T - 2, 0)
            yhi(T - 1, 1)

        def round_offset(dve, src, z, step, n0):
            nc.vector.tensor_scalar(z.bitcast(i32), src.bitcast(i32), 0x7F800000, 0x00400000,
                                    ALU.bitwise_and, ALU.bitwise_or).then_inc(step, 1)
            dve.wait_ge(step, n0 + 1)
            nc.vector.tensor_scalar(z, z, 1.5 * 2.0 ** -6, FP8_STEP, ALU.max, ALU.mult).then_inc(step, 1)
            dve.wait_ge(step, n0 + 2)
            nc.vector.tensor_tensor(src, src, z, ALU.add).then_inc(step, 1)

        def round_e4m3(dve, src, z, dst, step, n0, done):
            round_offset(dve, src, z, step, n0)
            dve.wait_ge(step, n0 + 3)
            nc.vector.tensor_tensor(dst, src, z, ALU.subtract).then_inc(done, 1)

        @block.vector
        def _(dve):
            dve.wait_ge(ld["wk"], 16)
            nc.vector.tensor_copy(wkp[:, 0, :], wkf).then_inc(wk_parts, 1)
            dve.wait_ge(wk_parts, 1)
            nc.vector.tensor_tensor(wkr, wkf, wkp[:, 0, :], ALU.subtract).then_inc(wk_parts, 1)
            dve.wait_ge(wk_parts, 2)
            nc.vector.tensor_copy(wkp[:, 1, :], wkr).then_inc(wk_parts, 1)
            dve.wait_ge(wk_parts, 3)
            nc.vector.tensor_tensor(wkp[:, 2, :], wkr, wkp[:, 1, :], ALU.subtract).then_inc(wk_parts, 1)
            dve.wait_ge(mlp_mm, 5)
            nc.vector.tensor_reduce(nmax, ps[3][0:B, 0:K], AX.X, ALU.max, negate=True).then_inc(mlp_ev, 1)
            dve.wait_ge(mlp_ev, 6)
            nc.vector.reciprocal(rinv, rsum).then_inc(mlp_ev, 1)
            dve.wait_ge(mlp_ev, 7)
            nc.vector.tensor_scalar(att, ex, rinv, None, ALU.mult).then_inc(mlp_ev, 1)
            thrice = lambda a: a.unsqueeze(1).to_broadcast([B, 3, K])
            dve.wait_ge(mlp_ev, 8)
            nc.vector.tensor_copy(attp[:, :, 0, :], thrice(att)).then_inc(att_parts, 1)
            dve.wait_ge(att_parts, 1)
            nc.vector.tensor_tensor(attr, att, attp[:, 0, 0, :], ALU.subtract).then_inc(att_parts, 1)
            dve.wait_ge(att_parts, 2)
            nc.vector.tensor_copy(attp[:, :, 1, :], thrice(attr)).then_inc(att_parts, 1)
            dve.wait_ge(att_parts, 3)
            nc.vector.tensor_tensor(attp[:, :, 2, :], thrice(attr), attp[:, :, 1, :], ALU.subtract)\
                .then_inc(att_parts, 1)

            def scales(vmax, inv, mul, src, step, n0):
                nc.vector.tensor_scalar(vmax, src, 1e-12, None, ALU.max).then_inc(step, 1)
                dve.wait_ge(step, n0 + 1)
                nc.vector.tensor_scalar(inv, vmax, 1.0 / FP8_MAX, None, ALU.mult).then_inc(step, 1)
                dve.wait_ge(step, n0 + 2)
                nc.vector.reciprocal(mul, inv).then_inc(step, 1)
                dve.wait_ge(step, n0 + 3)

            dve.wait_ge(mlp_ev, 10)
            nc.vector.tensor_copy(mixp[:, 0, :], mixb).then_inc(bias_parts, 1)
            dve.wait_ge(bias_parts, 1)
            nc.vector.tensor_tensor(mixr, mixb, mixp[:, 0, :], ALU.subtract).then_inc(bias_parts, 1)
            dve.wait_ge(bias_parts, 2)
            nc.vector.tensor_copy(mixp[:, 1, :], mixr).then_inc(bias_parts, 1)
            dve.wait_ge(bias_parts, 3)
            nc.vector.tensor_tensor(mixp[:, 2, :], mixr, mixp[:, 1, :], ALU.subtract).then_inc(bias_parts, 1)
            def largest_w0(h):
                dve.wait_ge(ld[f"f0_{h}"], 16)
                nc.vector.tensor_reduce(w_quarter[:, h:h + 1], w0f[:, 2 * h:2 * h + 2, :].rearrange("p r l -> p (r l)"),
                                        AX.X, ALU.max, apply_absolute_value=True).then_inc(w_red, 1)

            def place_odd(q):
                dve.wait_ge(mix_mm, q + 1)
                for b in range(NB):
                    ev = nc.vector.tensor_copy(mix_dst(q, 1, b), mix_src(q, 1, b))
                ev.then_inc(mix_odd, 1)

            def largest_mixed(t):
                dve.wait_ge(mixed_ev, 2 * t + 2)
                nc.vector.tensor_reduce(stat[:, bass.ds(t, 1)], slot_dyn(t + 2), AX.X, ALU.max,
                                        apply_absolute_value=True).then_inc(mixed_red, 1)

            dve.wait_ge(zeroed, 5)
            for q in range(4):
                place_odd(q)
            largest_w0(0)
            largest_mixed(0)
            largest_mixed(1)
            largest_w0(1)
            dve.wait_ge(ld["taps"], 16 * R8)
            tv = tapsf.rearrange("p o (h r) -> p h o r", h=2)
            for h in range(2):
                nc.vector.tensor_copy(taps16[:, 0, h, :, :], tv[:, h]).then_inc(taps_split, 1)
            dve.wait_ge(taps_split, 2)
            for h in range(2):
                nc.vector.tensor_tensor(taps16[:, 1, h, :, :], tv[:, h], taps16[:, 0, h, :, :], ALU.subtract)\
                    .then_inc(taps_split, 1)
            largest_mixed(2)
            largest_mixed(3)
            largest_w0(2)
            for t in range(4, 7):
                largest_mixed(t)
            largest_w0(3)
            dve.wait_ge(w_red, 4)
            nc.vector.tensor_reduce(w_part, w_quarter, AX.X, ALU.max).then_inc(w_red, 1)
            largest_mixed(7)
            largest_mixed(8)
            dve.wait_ge(w_pe, 1)
            nc.vector.tensor_reduce(w_all, ps[7][0:1, 0:P], AX.X, ALU.max).then_inc(w_red, 1)
            dve.wait_ge(w_pe, 2)
            scales(w_max, w_inv, w_mul, ps[7][:, 128:129], w_step, 0)
            for r in range(R8):
                if r >= 2:
                    dve.wait_ge(w0q[r % 2], r // 2)
                dve.wait_ge(w0v, r + 1)
                if r % 2:
                    round_e4m3(dve, w0f[:, r, :], wz[1], w0c[:, r, :], w_chain, 3 * r, w0q[1])
                else:
                    round_offset(dve, w0f[:, r, :], wz[0], w_chain, 3 * r)

            with dve.Fori(9, T - 1, 1) as i:
                largest_mixed(i)
            for h in range(2):
                dve.wait_ge(mixed_ev, 2 * T - 1 + h)
                nc.vector.tensor_reduce(amax_t[:, T - 1 + h:T + h], slot(T + 1)[:, h * H:(h + 1) * H], AX.X, ALU.max,
                                        apply_absolute_value=True).then_inc(mixed_red, 1)
            dve.wait_ge(mixed_red, T + 1)
            nc.vector.tensor_reduce(part_max, amax_t, AX.X, ALU.max).then_inc(mixed_red, 1)
            dve.wait_ge(x_pe, 1)
            nc.vector.tensor_reduce(x_all, ps[7][0:1, 0:P], AX.X, ALU.max).then_inc(mixed_red, 1)
            dve.wait_ge(x_pe, 2)
            scales(x_max, x_inv, x_mul, ps[7][:, 128:129], x_step, 0)
            nc.vector.tensor_tensor(acc_mul, x_inv, w_inv, ALU.mult).then_inc(x_step, 1)
            nc.vector.tensor_scalar(slot(2), slot(2), x_mul, None, ALU.mult).then_inc(x_step, 1)
            dve.wait_ge(x_step, 5)

            def quantise(t, n):
                if not (isinstance(t, int) and t == 0):
                    dve.wait_ge(q_done, t)
                    dve.wait_ge(v_done, t)
                round_e4m3(dve, slot_dyn(t + 2), qz, qT[n].rearrange("p k m -> p (k m)"), q_step, 3 * t, q_done)

            def residual0(t):
                v = slot_dyn(t).rearrange("p (s r) -> p r s", r=R8)
                dve.wait_ge(xb_done, t + 1)
                for h in range(2):
                    dve.wait_ge(f0_done, 2 * t + h + 1)
                    r = slice(4 * h, 4 * h + 4)
                    nc.vector.scalar_tensor_tensor(out=v[:, r, :], in0=ps[h][:, :].rearrange("p (r s) -> p r s", r=4),
                                                   scalar=acc_mul, in1=v[:, r, :], op0=ALU.mult, op1=ALU.add)\
                        .then_inc(x1_done, 1)

            def lo(t):
                v = slot_dyn(t).rearrange("p (s r) -> p r s", r=R8)
                for h in range(2):
                    dve.wait_ge(hi_done, 2 * t + h + 1)
                    r = slice(4 * h, 4 * h + 4)
                    s = slice(h, h + S)
                    nc.vector.tensor_tensor(split[:, r, s, 1], v[:, r, :], split[:, r, s, 0], ALU.subtract)\
                        .then_inc(lo_done, 1)

            def add_ctx(t, n, ge, first=False):
                dve.wait_ge(ld_ctx[n], ge)
                for b in range(NB):
                    dve.wait_ge(conv_done, 2 * t + b + 1)
                    if not first:
                        dve.wait_ge(yhi_done, 2 * t - 1 + b)
                        dve.wait_ge(ylo_done, 2 * t - 1 + b)
                    nc.vector.tensor_tensor(y1[:, b, :, :], ps[4 + b][:, :].rearrange("p (m r) -> p r m", r=R8),
                                            rowvec[:, n, b * C:(b + 1) * C].unsqueeze(1).to_broadcast([P, R8, C]),
                                            ALU.add).then_inc(y1_done, 1)

            def ylo(t, n):
                for b in range(NB):
                    dve.wait_ge(yhi_done, 2 * t + b + 1)
                    nc.vector.tensor_tensor(y1s[n][:, 1, :, b * C:(b + 1) * C], y1[:, b, :, :],
                                            y1s[n][:, 0, :, b * C:(b + 1) * C], ALU.subtract).then_inc(ylo_done, 1)

            def residual1(t, h):
                dve.wait_ge(x1b_done, t + 1)
                dve.wait_ge(f1_done, 2 * t + h + 1)
                v = Y[:, bass.ds(t * L + h * H, H)]
                nc.vector.tensor_tensor(v, ps[2 + h][:, :], v, ALU.add).then_inc(res_done, 1)

            quantise(0, 0)
            quantise(1, 1)
            residual0(0)
            lo(0)
            quantise(2, 0)
            residual0(1)
            lo(1)
            add_ctx(0, 0, 16, True)
            ylo(0, 0)

            def step(t, n, ctx_ge, more=True):
                residual0(t)
                lo(t)
                if more:
                    quantise(t + 1, 1 - n)
                residual1(t - 2, 0)
                add_ctx(t - 1, 1 - n, ctx_ge)
                ylo(t - 1, 1 - n)
                residual1(t - 2, 1)

            with dve.Fori(2, T - 2 - 1, 2) as i:
                step(i, 0, 8 * i)
                step(i + 1, 1, 8 * i + 16)
            step(T - 2, 0, 8 * (T - 2))
            step(T - 1, 1, 8 * (T - 2) + 16, False)
            residual1(T - 2, 0)
            add_ctx(T - 1, 1, 8 * T)
            ylo(T - 1, 1)
            residual1(T - 2, 1)
            residual1(T - 1, 0)
            residual1(T - 1, 1)

        @block.tensor
        def _(pe):
            mm = nc.tensor.matmul
            pe.wait_ge(ident_made, 1)
            pe.wait_ge(ld["mlp"], 160)
            nc.tensor.transpose(ps[0][:, 0:B], emb, ident[0:B, 0:B]).then_inc(mlp_mm, 1)
            nc.tensor.transpose(ps[7][:, 0:C], ctw, ident[0:C, 0:C]).then_inc(mlp_mm, 1)
            pe.wait_ge(mlp_ev, 1)
            mm(ps[1][:, 0:B], mw0, embT, start=True, stop=True).then_inc(mlp_mm, 1)
            pe.wait_ge(mlp_ev, 3)
            mm(ps[2][:, 0:B], mw1, h0T, start=True, stop=True).then_inc(mlp_mm, 1)
            pe.wait_ge(mlp_ev, 4)
            mm(ps[3][0:B, 0:K], h1T, mw2, start=True, stop=False)
            mm(ps[3][0:B, 0:K], ones[0:1, 0:B], rowb, start=False, stop=True).then_inc(mlp_mm, 1)
            pe.wait_ge(mlp_ev, 8)
            nc.tensor.transpose(ps[4][0:K, 0:B], att, ident[0:B, 0:B]).then_inc(mlp_mm, 1)
            pe.wait_ge(ident_cast, 1)
            pe.wait_ge(att_parts, 4)
            nc.tensor.transpose(ps[1][:, :].bitcast(bf16)[0:KP, 0:B], attp.rearrange("p j i k -> p (j i k)"),
                                ident_b[0:B, 0:B]).then_inc(attp_mm, 1)
            pe.wait_ge(mlp_ev, 9)
            mm(ps[5][0:B, 0:C], attT, mbk, start=True, stop=True).then_inc(mlp_mm, 1)
            mm(ps[6][0:B, 0:C], embT, ctwT, start=True, stop=False)
            mm(ps[6][0:B, 0:C], ones[0:1, 0:B], rowf, start=False, stop=True).then_inc(mlp_mm, 1)
            pe.wait_ge(ld["wkp"], 16)
            pe.wait_ge(attp_ev, 1)
            for q in range(4):
                for j in range(8):
                    o2 = 8 * q + j
                    last = mm(ps[q][:, j * B:(j + 1) * B], wkp9[:, o2 * 2 * C:(o2 + 1) * 2 * C],
                              attpT, start=True, stop=True)
                last.then_inc(mix_mm, 1)
            pe.wait_ge(mlp_ev, N_MLP)

            def keep_clock(count, lhsT, rhs):
                for _ in range(count):
                    mm(ps[6][:, :], lhsT, rhs, start=True, stop=True)

            keep_clock(5, wkp9[:, 0:P], wkp9[:, 0:H])
            pe.wait_ge(mix_even, 4)
            pe.wait_ge(mix_odd, 4)
            pe.wait_ge(zeroed, 5)

            def mixed_products(t, n, h, first=False):
                m = n % 2
                if not first:
                    pe.wait_ge(mixed_ev, 2 * t + h - 3)
                for k in range(4):
                    j = 4 * h + k
                    mm(ps[2 * m + h][:, k * P:(k + 1) * P], xring[n][:, j * P:(j + 1) * P],
                       mixw_dyn(t), start=(k == 0), stop=False, skip_group_check=True)

            def mixed_bias(n, h):
                mm(ps[2 * (n % 2) + h][:, :].rearrange("p (k m) -> p k m", m=P), ones_b,
                   rowb3[:, n, :].unsqueeze(1).to_broadcast([3, H // P, P]), start=False, stop=True,
                   skip_group_check=True).then_inc(mixed, 1)

            def mixed_tile(t, n, ge, between=None):
                pe.wait_ge(ld_x[n], ge)
                pe.wait_ge(ld_rb[n], ge)
                for h in range(2):
                    mixed_products(t, n, h)
                    mixed_bias(n, h)
                    if h == 0 and between is not None:
                        between()

            def turned(m, dt, src, idt, at, ready, ge):
                pe.wait_ge(ready, ge)
                if at is not None:
                    pe.wait_ge(wT_ev, at)
                pb = ps[4 + m][:, :].bitcast(dt)
                for k in range(KT):
                    last = nc.tensor.transpose(pb[:, k * P:(k + 1) * P], src(k), idt)
                last.then_inc(wT_mm, 1)

            def turned0(r):
                turned(r % 4, bf16, lambda k: w0c_dyn(r, k), ident_b, r - 3 if r > 3 else None, w0q[r % 2],
                       r // 2 + 1)

            def turned1(n):
                turned(n % 4, fp16, lambda k: w1c_dyn(n, k), ident_h, KT + n - 3, w1d, n + 1)

            for n in range(2):
                pe.wait_ge(ld_x[n], 16)
                for h in range(2):
                    mixed_products(n, n, h, first=True)
            for n in range(2):
                pe.wait_ge(ld_rb[n], 16)
                for h in range(2):
                    mixed_bias(n, h)
            with pe.Fori(2, 10 - 3, 4) as i:
                for k in range(4):
                    mixed_tile(i + k, (2 + k) % 4, 4 * i + (8 if k < 2 else 24))
            pe.wait_ge(w_red, 5)
            nc.tensor.transpose(ps[7][0:1, 0:P], w_part, ident[:, :]).then_inc(w_pe, 1)

            def spread_w_max():
                pe.wait_ge(w_red, 6)
                mm(ps[7][:, 128:129], ones, w_all, start=True, stop=True).then_inc(w_pe, 1)

            mixed_tile(10, 2, 48, spread_w_max)
            for t in range(11, 16):
                mixed_tile(t, t % 4, 16 * (t // 4) + 16)
            pe.wait_ge(ident_cast, 2)
            pe.wait_ge(w_step, 3)
            for r in range(R8):
                mixed_tile(16 + r, r % 4, 16 * (r // 4) + 80)
                turned0(r)
            for n in range(KT - 1):
                mixed_tile(24 + n, n % 4, 16 * (n // 4) + 112)
                turned1(n)
            turned1(KT - 1)
            mixed_tile(T - 1, 3, 128)
            pe.wait_ge(mixed_red, T + 2)
            pe.wait_ge(wT_ev, 2 * KT)
            nc.tensor.transpose(ps[7][0:1, 0:P], part_max, ident[:, :]).then_inc(x_pe, 1)
            pe.wait_ge(mixed_red, T + 3)
            mm(ps[7][:, 128:129], ones, x_all, start=True, stop=True).then_inc(x_pe, 1)
            pe.wait_ge(taps_split, 4)
            keep_clock(18, f0T[:, 0, 0:P], f0T[:, 0, 0:H])

            def ffn0(t, n, first=False):
                pe.wait_ge(q_done, t + 1)
                for h in range(2):
                    if not first:
                        pe.wait_ge(x1_done, 2 * t - 1 + h)
                    for k in range(KT):
                        last = mm(ps[h][:, :], qT[n][:, k, :], f0T[:, k, h * H:(h + 1) * H],
                                  start=(k == 0), stop=(k == KT - 1))
                    last.then_inc(f0_done, 1)

            def conv(t, first=False):
                pe.wait_ge(split_in, 16 * t + 16)
                for b in range(NB):
                    if not first:
                        pe.wait_ge(y1_done, 2 * t - 1 + b)
                    for g in range(G):
                        parts = [(xp, wp, h) for xp, wp in ((0, 0), (0, 1), (1, 0)) for h in range(2)]
                        for j, (xp, wp, h) in enumerate(parts):
                            last = mm(ps[4 + b][:, g * P:(g + 1) * P], convin[:, b * G + g, h:h + S, xp],
                                      taps16[:, wp, h, g * CG:(g + 1) * CG, :].rearrange("p a b -> p (a b)"),
                                      start=(j == 0), stop=(j == len(parts) - 1))
                    last.then_inc(conv_done, 1)

            def ffn1(t, n, h, first=False):
                pe.wait_ge(ylo_done, 2 * t + 2)
                if not first:
                    pe.wait_ge(res_done, 2 * t - 1 + h)
                for e in range(2):
                    for k in range(KT):
                        last = mm(ps[2 + h][:, :], y1s[n][:, e, k, :], f1T[:, k, h * H:(h + 1) * H],
                                  start=(e == 0 and k == 0), stop=(e == 1 and k == KT - 1))
                last.then_inc(f1_done, 1)

            ffn0(0, 0, True)
            ffn0(1, 1)
            keep_clock(8, f0T[:, 0, 0:P], f0T[:, 0, 0:H])
            ffn0(2, 0)
            conv(0, True)
            keep_clock(10, f0T[:, 0, 0:P], f0T[:, 0, 0:H])

            def step(t, n, first=False):
                if not first:
                    ffn0(t, n)
                ffn1(t - 2, n, 0, first)
                conv(t - 1)
                ffn1(t - 2, n, 1, first)

            step(2, 0, True)
            step(3, 1)
            with pe.Fori(4, T - 1, 2) as i:
                step(i, 0)
                step(i + 1, 1)
            ffn1(T - 2, 0, 0)
            conv(T - 1)
            ffn1(T - 2, 0, 1)
            ffn1(T - 1, 1, 0)
            ffn1(T - 1, 1, 1)



_INS = ['x', 'cond_128', 'fside_S_0', 'L0_cond_W0', 'L0_cond_b0', 'L0_cond_W1', 'L0_cond_b1', 'L0_cond_W2',
        'L0_cond_b2', 'L0_cond_weight', 'L0_cond_bias_k', 'L0_ffn_weight', 'L0_ffn_bias', 'L1_cond_weight',
        'L1_cond_c_weight', 'L1_ffn_W_q', 'L1_ffn_scale', 'L1_ffn_zero', 'L1_ffn_bias']


def kernel(**inputs):
    import numpy as _np
    import concourse.bacc as _bacc
    from concourse import mybir as _mybir
    from concourse.bass_utils import run_bass_kernel_spmd as _run

    nc = _bacc.Bacc("TRN2", target_bir_lowering=False, num_devices=1)
    arrays, args = {}, []
    for name in _INS:
        a = _np.ascontiguousarray(inputs[name])
        arrays[f"in_{name}_dram"] = a
        args.append(nc.dram_tensor(f"in_{name}_dram", a.shape, _mybir.dt.from_np(a.dtype), kind="ExternalInput").ap())
    out = nc.dram_tensor("out_dram", inputs['x'].shape, _mybir.dt.float32, kind="ExternalOutput").ap()
    adaln_ffn_kernel(nc, *args, out)
    return _run(nc, [arrays], core_ids=[0]).results[0]["out_dram"]
```
